# Optimizing a Trainium2 kernel written in Bass

```python
import numpy as np
import jax
import jax.numpy as jnp

def _softmax(x, axis=-1):
    return jax.nn.softmax(x, axis=axis)

def _gelu(x):
    return jax.nn.gelu(x, approximate=True)

def _silu(x):
    return jax.nn.silu(x)

def _sigmoid(x):
    return jax.nn.sigmoid(x)

def _layernorm(x, axis=-1, eps=1e-05):
    m = jnp.mean(x, axis=axis, keepdims=True)
    v = jnp.var(x, axis=axis, keepdims=True)
    return (x - m) / jnp.sqrt(v + eps)

def _scatter_add(tgt, idx, src, axis=0):
    return tgt.at[idx].add(src)

def _segment_sum(src, seg, n):
    return jax.ops.segment_sum(src, seg, n)
kernel_name = 'mk_adaln_d1_jaxref_r8_30023c'

def setup_inputs(seed: int=0):
    np.random.seed(seed)
    _w = jnp.asarray

    def _L0_attn_setup():
        import jax, jax.numpy as jnp
        import numpy as np
        from jax import lax
        BLOCK_LEN = 128
        NEG_INF = -1000000000.0
        key = jax.random.key(seed)
        ks = jax.random.split(key, 8)
        N, L, Dm = (2, 1024, 512)
        W, H, dh = (128, 16, 64)
        s = lambda fan: 1.0 / np.sqrt(fan)
        return {'inputs': jax.random.normal(ks[0], (N, L, Dm), jnp.float32), 'conv_w': jax.random.normal(ks[1], (3, Dm, 3 * W), jnp.float32) * s(3 * Dm), 'conv_b': jnp.zeros((3 * W,), jnp.float32), 'wq': jax.random.normal(ks[2], (W, H, dh), jnp.float32) * s(W), 'bq': jnp.zeros((H, dh), jnp.float32), 'wk': jax.random.normal(ks[3], (W, H, dh), jnp.float32) * s(W), 'bk': jnp.zeros((H, dh), jnp.float32), 'wv': jax.random.normal(ks[4], (W, H, dh), jnp.float32) * s(W), 'bv': jnp.zeros((H, dh), jnp.float32), 'wo': jax.random.normal(ks[5], (H, dh, W), jnp.float32) * s(H * dh), 'bo': jnp.zeros((W,), jnp.float32), 'proj_w': jax.random.normal(ks[6], (W, Dm), jnp.float32) * s(W), 'proj_b': jnp.zeros((Dm,), jnp.float32)}
    _L0_attn_in = _L0_attn_setup()

    def _L0_ffn_setup():
        import jax, jax.numpy as jnp
        import numpy as np
        TOP_K = 2
        SCALING = 32.0 / 64.0
        key = jax.random.key(seed)
        ks = jax.random.split(key, 6)
        Bsz, S, Din, Dout, R, E = (4, 256, 512, 512, 64, 16)
        x = jax.random.normal(ks[0], (Bsz, S, Din), dtype=jnp.float32)
        base_w = jax.random.normal(ks[1], (Dout, Din), dtype=jnp.float32) * 0.02
        base_b = jax.random.normal(ks[2], (Dout,), dtype=jnp.float32) * 0.02
        A = jax.random.normal(ks[3], (R, Din), dtype=jnp.float32) * (1.0 / np.sqrt(Din))
        B = jax.random.normal(ks[4], (E, Dout, R), dtype=jnp.float32) * 0.02
        router_w = jax.random.normal(ks[5], (E, Din), dtype=jnp.float32) * 0.02
        return {'x': x, 'base_w': base_w, 'base_b': base_b, 'A': A, 'B': B, 'router_w': router_w}
    _L0_ffn_in = _L0_ffn_setup()
    _L0_c = _w((lambda *s: np.random.randn(*s).astype(np.float32) * 0.05)(2, 512))
    _L0_wmod = _w((lambda *s: np.random.randn(*s).astype(np.float32) * 0.05)(512, 6 * 512) * 512 ** (-0.5))
    _d = {'L0_attn_inputs': _L0_attn_in['inputs'], 'L0_attn_conv_w': _L0_attn_in['conv_w'], 'L0_attn_conv_b': _L0_attn_in['conv_b'], 'L0_attn_wq': _L0_attn_in['wq'], 'L0_attn_bq': _L0_attn_in['bq'], 'L0_attn_wk': _L0_attn_in['wk'], 'L0_attn_bk': _L0_attn_in['bk'], 'L0_attn_wv': _L0_attn_in['wv'], 'L0_attn_bv': _L0_attn_in['bv'], 'L0_attn_wo': _L0_attn_in['wo'], 'L0_attn_bo': _L0_attn_in['bo'], 'L0_attn_proj_w': _L0_attn_in['proj_w'], 'L0_attn_proj_b': _L0_attn_in['proj_b'], 'L0_ffn_base_w': _L0_ffn_in['base_w'], 'L0_ffn_base_b': _L0_ffn_in['base_b'], 'L0_ffn_A': _L0_ffn_in['A'], 'L0_ffn_B': _L0_ffn_in['B'], 'L0_ffn_router_w': _L0_ffn_in['router_w'], 'L0_c': _L0_c, 'L0_wmod': _L0_wmod}
    _x0 = _d['L0_attn_inputs']
    _d['L0_attn_inputs'] = jax.random.normal(jax.random.fold_in(jax.random.key(seed), 1), (2, 1024, 512), dtype=_x0.dtype)
    del _x0
    return _d

def reference(L0_attn_inputs, L0_attn_conv_w, L0_attn_conv_b, L0_attn_wq, L0_attn_bq, L0_attn_wk, L0_attn_bk, L0_attn_wv, L0_attn_bv, L0_attn_wo, L0_attn_bo, L0_attn_proj_w, L0_attn_proj_b, L0_ffn_base_w, L0_ffn_base_b, L0_ffn_A, L0_ffn_B, L0_ffn_router_w, L0_c, L0_wmod):

    def _L0_attn_ref(inputs, conv_w, conv_b, wq, bq, wk, bk, wv, bv, wo, bo, proj_w, proj_b):
        import jax, jax.numpy as jnp
        import numpy as np
        from jax import lax
        BLOCK_LEN = 128
        NEG_INF = -1000000000.0
        N, L, Dm = inputs.shape
        x = lax.conv_general_dilated(inputs, conv_w, window_strides=(1,), padding='SAME', dimension_numbers=('NWC', 'WIO', 'NWC')) + conv_b
        q, k, v = jnp.split(x, 3, axis=-1)
        W_ = q.shape[-1]
        nb = L // BLOCK_LEN
        q = q.reshape(N * nb, BLOCK_LEN, W_)
        k = k.reshape(N * nb, BLOCK_LEN, W_)
        v = v.reshape(N * nb, BLOCK_LEN, W_)
        dh = wq.shape[-1]
        qh = jnp.einsum('btd,dhe->bthe', q, wq) + bq
        kh = jnp.einsum('btd,dhe->bthe', k, wk) + bk
        vh = jnp.einsum('btd,dhe->bthe', v, wv) + bv
        scale = 1.0 / jnp.sqrt(jnp.asarray(dh, qh.dtype))
        scores = jnp.einsum('bqhe,bkhe->bhqk', qh * scale, kh)
        causal = jnp.tril(jnp.ones((BLOCK_LEN, BLOCK_LEN), bool))
        scores = jnp.where(causal, scores, NEG_INF)
        p = jax.nn.softmax(scores, axis=-1)
        o = jnp.einsum('bhqk,bkhe->bqhe', p, vh)
        o = jnp.einsum('bqhe,hed->bqd', o, wo) + bo
        o = o.reshape(N, L, W_)
        return o @ proj_w + proj_b

    def _L0_ffn_ref(x, base_w, base_b, A, B, router_w):
        import jax, jax.numpy as jnp
        import numpy as np
        TOP_K = 2
        SCALING = 32.0 / 64.0
        base_out = jnp.einsum('bsi,oi->bso', x, base_w) + base_b
        res_hidden = jnp.einsum('bsi,ri->bsr', x, A)
        logits = jnp.einsum('bsi,ei->bse', x, router_w)
        probs = jax.nn.softmax(logits, axis=-1)
        topw, topi = jax.lax.top_k(probs, TOP_K)
        topw = topw / (jnp.sum(topw, axis=-1, keepdims=True) + 1e-06)
        num_experts = B.shape[0]
        combine = jnp.sum(jax.nn.one_hot(topi, num_experts, dtype=x.dtype) * topw[..., None], axis=-2)
        delta = jnp.einsum('bse,bsr,eor->bso', combine, res_hidden, B)
        return base_out + delta * SCALING
    x = L0_attn_inputs
    mod = (_silu(L0_c) @ L0_wmod).reshape(L0_c.shape[0], 6, 1, -1)
    sa, ca, ga, sb, cb, gb = (mod[:, 0], mod[:, 1], mod[:, 2], mod[:, 3], mod[:, 4], mod[:, 5])
    ga = (2 * (ga >= 0) - 1) * jnp.maximum(jnp.abs(ga), 0.25)
    gb = (2 * (gb >= 0) - 1) * jnp.maximum(jnp.abs(gb), 0.25)
    h = _layernorm(x, axis=-1) * (1 + ca) + sa
    x = x + ga * _L0_attn_ref(h, L0_attn_conv_w, L0_attn_conv_b, L0_attn_wq, L0_attn_bq, L0_attn_wk, L0_attn_bk, L0_attn_wv, L0_attn_bv, L0_attn_wo, L0_attn_bo, L0_attn_proj_w, L0_attn_proj_b)
    h = _layernorm(x, axis=-1) * (1 + cb) + sb
    x = x + gb * _L0_ffn_ref(h, L0_ffn_base_w, L0_ffn_base_b, L0_ffn_A, L0_ffn_B, L0_ffn_router_w)
    return x

_drawn_inputs = setup_inputs


def setup_inputs(seed=0):
    import zlib

    import numpy as np

    out = dict(_drawn_inputs(seed))
    spreads = {'L0_attn_conv_b': (0.0, 0.302),
     'L0_attn_bq': (0.0, 0.8),
     'L0_attn_bk': (0.0, 0.8),
     'L0_attn_bv': (0.0, 0.324),
     'L0_attn_bo': (0.0, 0.328),
     'L0_attn_proj_b': (0.0, 0.311)}
    factors = {'L0_ffn_base_b': 8.0, 'L0_ffn_A': 4.006, 'L0_ffn_B': 4.011, 'L0_ffn_router_w': 4.258}
    for name, (base, spread) in spreads.items():
        noise = np.random.default_rng([zlib.crc32(name.encode()), seed]).standard_normal(out[name].shape)
        drawn = base * np.exp(spread * noise) if base else spread * noise
        out[name] = jnp.asarray(drawn.astype(out[name].dtype))
    for name, factor in factors.items():
        out[name] = (out[name] * factor).astype(out[name].dtype)
    return out
```

```python
from contextlib import ExitStack

import concourse.bass as bass
from concourse import mybir

ALU = mybir.AluOpType
ACT = mybir.ActivationFunctionType
AX = mybir.AxisListType
F32 = mybir.dt.float32
F32R = mybir.dt.float32r
F16 = mybir.dt.float16
BF16 = mybir.dt.bfloat16
U32 = mybir.dt.uint32

P = 128
EPS = 1e-5
NEG = -1e9
HI, LO = 0, 1
PASSES = [(HI, HI), (HI, LO), (LO, HI)]


class Tally:

    def __init__(self, sem):
        self.sem, self.before, self.k = sem, 0, 0

    def at(self, before):
        self.before, self.k = before, 0

    def inc(self, instruction):
        self.k += 1
        return instruction.then_inc(self.sem, 1)

    def now(self):
        return self.before + self.k


def bass_adaln_block(nc, x, conv_w, conv_b, wq, bq, wk, bk, wv, bv, wo, bo, proj_w, proj_b,
                     base_w, base_b, lora_a, lora_b, router_w, cond, wmod, out):
    NB, L, D = x.shape
    TAPS, _, C3 = conv_w.shape
    W = C3 // 3
    _, H, DH = wq.shape
    HE = H * DH
    E, _, R = lora_b.shape
    DC = D // P
    NC = HE // P
    CH = 2 * P
    NCH = NB * L // CH
    CPB = L // CH
    NBLK = NB * L // P
    BPB = L // P
    ER = E * R // P
    ARW = R + E
    assert W == P and D == 4 * P and 2 * DH == P and 2 * R == P

    W_CONV, W_QKPV, W_V, W_WO, W_PROJ, W_N = 0, 3, 15, 19, 20, 22
    T_PT, T_OT, T_LN, T_N = 0, 8, 12, 14
    W0 = 3 + 8 + 4
    T0 = 6

    xin = x.rearrange("n (c b p) d -> (n c) p b d", p=P, b=2)
    x1_chunk = out.rearrange("n (c b p) d -> (n c) p b d", p=P, b=2)
    x1_block = out.rearrange("n (b p) d -> (n b) p d", p=P)

    with ExitStack() as ctx:
        def sem(name):
            return ctx.enter_context(nc.semaphore(name))

        def psum(name, shape=(P, 512), dt=F32):
            return ctx.enter_context(nc.psum_tensor(name, list(shape), dt))

        slab = ctx.enter_context(nc.sbuf_tensor("slab", [P, 53200], F32))
        first = nc.sbuf_base - 4 * 53200
        place = [first]

        def put(name, shape, dt, at=None):
            size = {F32: 4, F32R: 4, F16: 2, BF16: 2, U32: 4}[dt]
            n = size
            for s in shape[1:]:
                n *= s
            where = place[0] if at is None else at
            t = nc.alloc_sbuf_tensor_at(name, list(shape), dt, offset=where)
            if at is None:
                place[0] += (n + 31) // 32 * 32
            return t, where

        cw, cw_at = put("cw", [P, 2, TAPS, DC, C3], F32R)
        pw, pw_at = put("pw", [P, 2, 3, HE], F32R)
        hT, _ = put("hT", [P, 2, 2, DC, CH + 2], F32R)
        f_end = place[0]
        wow, wow_at = put("wow", [P, 2, NC, W], F32R)
        pjw, pjw_at = put("pjw", [P, 2, D], F32R)
        common = place[0]
        cv, _ = put("cv", [P, 3, 2, CH], F32R)
        qk16, qk16_at = put("qk16", [P, 2, 2 * NC, CH], F16)
        v16, _ = put("v16", [P, 2, 2, HE], F16)
        prob, prob_at = put("prob", [P, 4, 8, P], F32)
        pt16, _ = put("pt16", [P, 2, 2, 8, P], F16)
        o, _ = put("o", [P, 2, HE], F32)
        oT, _ = put("oT", [P, 2, NC, CH], F32R)
        att, _ = put("att", [P, 2, CH], F32R)
        xln, _ = put("xln", [P, 2, D], F32)
        xn, _ = put("xn", [P, 2, D], F32)
        hf, _ = put("hf", [P, DC, CH], F32)
        xr, xr_at = put("xr", [P, 2, D], F32)
        x1, _ = put("x1", [P, 2, D], F32)
        gaB, _ = put("gaB", [P, NB, D], F32)
        gaPB, _ = put("gaPB", [P, NB, D], F32)
        ident, _ = put("ident", [P, P], F32)
        ident16, _ = put("ident16", [P, P], BF16)
        mask, _ = put("mask", [P, 4, P], BF16)
        modT, _ = put("modT", [P, 4, DC, NB], F32)
        gbrow, _ = put("gbrow", [NB, D], F32)
        pick, _ = put("pick", [NB, NB, P], F32)
        keep, _ = put("keep", [P, NCH + 2, 2 * DC], F32)
        half, _ = put("half", [P, 2], F32)
        cb, _ = put("cb", [P, 3], F32)
        bqk, _ = put("bqk", [P, 2 * NC], F32)
        bvT, _ = put("bvT", [P, NC], F32)
        boT, _ = put("boT", [P, 1], F32)
        bofs, _ = put("bofs", [P, 1], F32)
        silT, _ = put("silT", [P, 4, DC, NB], F32)
        st, _ = put("st", [P, 2, 6], F32)
        mv, _ = put("mv", [P, 2, 2], F32)
        rs, _ = put("rs", [P, 5, 2], F32)
        nm, _ = put("nm", [P, 4, 8], F32)
        rsum, _ = put("rsum", [P, 4, 8], F32)
        rinv, _ = put("rinv", [P, 4, 8], F32)
        iota, _ = put("iota", [P, E], F32)
        tmprow, _ = put("tmprow", [NB, 2, D], F32)
        assert place[0] <= nc.sbuf_base
        cw_raw, _ = put("cw_raw", [P, TAPS, DC, C3], F32, at=cw_at + 4 * TAPS * DC * C3)
        pw_raw, _ = put("pw_raw", [P, 3, HE], F32, at=pw_at + 4 * 3 * HE)
        wow_raw, _ = put("wow_raw", [P, NC, W], F32, at=wow_at + 4 * NC * W)
        pjw_raw, _ = put("pjw_raw", [P, D], F32, at=pjw_at + 4 * D)
        wm, _ = put("wm", [P, DC, 6, D], F32, at=prob_at)
        sarow, _ = put("sarow", [NB, 2, D], F32, at=qk16_at)
        garow, _ = put("garow", [NB, 3, D], F32, at=xr_at)
        brow, _ = put("brow", [1, D], F32, at=xr_at + 4 * 3 * D)
        mrow = [sarow[:, 0], sarow[:, 1], garow[:, 0], garow[:, 1], garow[:, 2], gbrow[:]]
        place[0] = cw_at
        btw, _ = put("btw", [P, 2, ER, D], F32R)
        bsw, _ = put("bsw", [P, 2, DC, D], F32R)
        arT, _ = put("arT", [P, DC, ARW], F32)
        braw, _ = put("braw", [P, DC, E, R], F32)
        bsraw, _ = put("bsraw", [P, DC, D], F32)
        arraw, _ = put("arraw", [ARW, D], F32)
        assert place[0] <= f_end
        place[0] = common
        x2, _ = put("x2", [P, 4, D], F32)
        xn2, _ = put("xn2", [P, D], F32)
        hf2, _ = put("hf2", [P, 2, DC, P], F32)
        h2, _ = put("h2", [P, 2, 2, DC, P], F32R)
        res, _ = put("res", [P, R], F32)
        G, _ = put("G", [P, E, R], F32)
        gT, _ = put("gT", [P, 2, 2, ER, P], F32R)
        ob, _ = put("ob", [P, 2, D], F32)
        gbB, _ = put("gbB", [P, NB, D], F32)
        gbBB, _ = put("gbBB", [P, NB, D], F32)
        brow2, _ = put("brow2", [1, D], F32)
        top, _ = put("top", [P, 8], F32)
        topi, _ = put("topi", [P, 8], U32)
        topf, _ = put("topf", [P, 2], F32)
        ng, _ = put("ng", [P, 1], F32)
        ex, _ = put("ex", [P, E], F32)
        zz, _ = put("zz", [P, 8], F32)
        cmb, _ = put("cmb", [P, 2, E], F32)

        S = [psum(f"S{i}") for i in range(4)]
        WB = [psum(f"W{i}") for i in range(2)]
        TB = [psum(f"T{i}") for i in range(2)]

        dma_names = ["c", "xa", "wm0", "wm1", "cw", "pq", "pk", "pv", "wo", "pj", "small", "x", "xr",
                     "raw", "x2a", "x2b", "x2c", "x2d", "brow2"]
        ld = {n: sem("ld_" + n) for n in dma_names}
        x1_stored, out_stored0, out_stored1 = sem("x1_stored"), sem("out_stored0"), sem("out_stored1")
        w_full, w_done, t_full, t_done, s_full, s_done = (
            sem(n) for n in ("w_full", "w_done", "t_full", "t_done", "s_full", "s_done"))
        m_full, m_done = sem("m_full"), sem("m_done")
        sil_exp, sil_done, split_hi, split_lo = (
            sem(n) for n in ("sil_exp", "sil_done", "split_hi", "split_lo"))
        var_ready, rstd_ready, xn_ready, h_hi, h_ready = (
            sem(n) for n in ("var_ready", "rstd_ready", "xn_ready", "h_hi", "h_ready"))
        pool_chain, dve_chain = sem("pool_chain"), sem("dve_chain")
        cv_hi, qk_hi, v_hi, pt_hi, ot_hi, att_hi = (
            sem(n) for n in ("cv_hi", "qk_hi", "v_hi", "pt_hi", "ot_hi", "att_hi"))
        nm_ready, xr_biased, x1_ready = sem("nm_ready"), sem("xr_biased"), sem("x1_ready")
        o_full, o_done, a_full, a_done, l_full, l_done, g_full, g_done = (
            sem(n) for n in ("o_full", "o_done", "a_full", "a_done", "l_full", "l_done", "g_full", "g_done"))
        prep_hi, var2_ready, rstd2_ready, xn2_ready, h2_hi, h2_ready = (
            sem(n) for n in ("prep_hi", "var2_ready", "rstd2_ready", "xn2_ready", "h2_hi", "h2_ready"))
        x2_biased, ng_ready, ex_done, g_ready, gt_hi, ob_ready = (
            sem(n) for n in ("x2_biased", "ng_ready", "ex_done", "g_ready", "gt_hi", "ob_ready"))
        ld_x2 = [ld["x2a"], ld["x2b"], ld["x2c"], ld["x2d"]]
        out_stored = [out_stored0, out_stored1]

        w_at = lambda t, k: W0 + W_N * t + k
        t_at = lambda t, k: T0 + T_N * t + k
        NEWTON = 5
        N_MOD = 6 + 1 + NB + NB + 1
        N_PREP = ER + DC + 1 + 2 * NB

        splits = [(cw[:, :, i], cw_raw[:, i], 1.0, ld["cw"]) for i in range(TAPS)]
        splits += [(pw[:, :, 0], pw_raw[:, 0], DH ** -0.5, ld["pq"]), (pw[:, :, 1], pw_raw[:, 1], 1.0, ld["pk"]),
                   (pw[:, :, 2], pw_raw[:, 2], 1.0, ld["pv"]), (wow, wow_raw, 1.0, ld["wo"]),
                   (pjw, pjw_raw, 1.0, ld["pj"])]
        N_SPLIT = len(splits)
        N_CONST = 11 + len(range(0, NCH + 2, CPB))
        SMALL = 6

        block = ctx.enter_context(nc.Block())

        @block.sync
        def _(sp):
            sp.dma_start(xln[:], xin[0]).then_inc(ld["x"], 16)
            for n in range(2):
                lo, hi = (0, 2) if n == 0 else (2, 6)
                sp.dma_start(wm[:, :, lo:hi, :], wmod.rearrange("(k p) (m d) -> p k m d", p=P, m=6)[:, :, lo:hi, :]
                             ).then_inc(ld[f"wm{n}"], 16)
                if n == 0:
                    sp.dma_start(cw_raw[:], conv_w.rearrange("t (c p) o -> p t c o", p=P)).then_inc(ld["cw"], 16)
                    for i, (w, name) in enumerate(((wq, "pq"), (wk, "pk"), (wv, "pv"))):
                        sp.dma_start(pw_raw[:, i, :], w.rearrange("d h e -> d (h e)")).then_inc(ld[name], 16)
            sp.dma_start(wow_raw[:], wo.rearrange("h e d -> (h e) d").rearrange("(c p) d -> p c d", p=P)
                         ).then_inc(ld["wo"], 16)
            sp.dma_start(pjw_raw[:], proj_w).then_inc(ld["pj"], 16)
            for j in range(1, 3):
                sp.wait_ge(xn_ready, 2 * j)
                sp.dma_start(xln[:], xin[j]).then_inc(ld["x"], 16)
            sp.wait_ge(m_done, N_MOD)
            sp.dma_start(xr[:], xin[0]).then_inc(ld["xr"], 16)

            with sp.Fori(0, NCH - 1) as t:
                sp.wait_ge(xn_ready, 2 * t + 6)
                sp.dma_start(xln[:], xin[bass.ds((t + 3) % NCH, 1)].rearrange("a p b d -> p (a b) d")
                             ).then_inc(ld["x"], 16)
                sp.wait_ge(x1_ready, 2 * t + 2)
                sp.dma_start(x1_chunk[bass.ds(t, 1)].rearrange("a p b d -> p (a b) d"), x1[:]
                             ).then_inc(x1_stored, 16)
                sp.wait_ge(x1_stored, 16 * t + 16)
                sp.dma_start(xr[:], xin[bass.ds(t + 1, 1)].rearrange("a p b d -> p (a b) d")
                             ).then_inc(ld["xr"], 16)
            sp.wait_ge(w_full, w_at(NCH - 2, W_N))
            sp.wait_ge(h_ready, 3 * (NCH + 2))
            sp.dma_start(bsraw[:], base_w.rearrange("(c p) i -> p c i", p=P)).then_inc(ld["raw"], 16)
            sp.dma_start(arraw[0:R, :], lora_a).then_inc(ld["raw"], 16)
            sp.dma_start(arraw[R:ARW, :], router_w).then_inc(ld["raw"], 16)
            for c in range(DC):
                sp.dma_start(braw[:, c], lora_b[:, c * P:(c + 1) * P, :].rearrange("e p r -> p e r")
                             ).then_inc(ld["raw"], 16)
            sp.wait_ge(x1_ready, 2 * NCH)
            sp.dma_start(x1_chunk[NCH - 1], x1[:]).then_inc(x1_stored, 16)

            sp.wait_ge(x1_stored, 16 * NCH)
            sp.dma_start(brow2[:], base_b.rearrange("(a d) -> a d", a=1)).then_inc(ld["brow2"], 16)
            for i in range(4):
                sp.dma_start(x2[:, i, :], x1_block[i]).then_inc(ld_x2[i], 16)
            with sp.Fori(0, NBLK // 4) as it:
                for q in range(4):
                    i = 4 * it + q
                    sp.wait_ge(ob_ready, i + 1)
                    sp.dma_start(x1_block[bass.ds(i, 1)].rearrange("a p d -> (a p) d"), ob[:, q % 2, :]
                                 ).then_inc(out_stored[q % 2], 16)
                    sp.wait_ge(out_stored[q % 2], 16 * (2 * it + q // 2 + 1))
                    sp.dma_start(x2[:, q, :], x1_block[bass.ds((i + 4) % NBLK, 1)].rearrange("a p d -> (a p) d")
                                 ).then_inc(ld_x2[q], 16)
            for q in range(4):
                sp.wait_ge(ld_x2[q], 16 * (NBLK // 4 + 1))

        @block.gpsimd
        def _(pool):
            for b in range(NB):
                pool.dma_start(silT[:, 0, :, b], cond[b].rearrange("(k p) -> p k", p=P),
                               allow_slow_non_contiguous=True).then_inc(ld["c"], 16)
            small = [(cb[:], conv_b.rearrange("(o p) -> p o", p=P)),
                     (bqk[:, 0:NC], bq.rearrange("(c two) e -> (two e) c", two=2)),
                     (bqk[:, NC:], bk.rearrange("(c two) e -> (two e) c", two=2)),
                     (bvT[:], bv.rearrange("(c two) e -> (two e) c", two=2)),
                     (boT[:], bo.rearrange("(p a) -> p a", a=1)),
                     (brow[:], proj_b.rearrange("(a d) -> a d", a=1))]
            assert len(small) == SMALL
            for dst, src in small:
                pool.dma_start(dst, src, allow_slow_non_contiguous=True).then_inc(ld["small"], 16)
            chain = Tally(pool_chain)

            def link(instruction):
                chain.inc(instruction)
                pool.wait_ge(pool_chain, chain.now())

            link(nc.gpsimd.memset(ident[:], 0.0))
            link(nc.gpsimd.affine_select(out=ident[:], in_=ident[:], compare_op=ALU.not_equal, fill=1.0, base=0,
                                         pattern=[[-1, P]], channel_multiplier=1))
            link(nc.gpsimd.tensor_copy(ident16[:], ident[:]))
            link(nc.gpsimd.memset(mask[:], 0.0))
            link(nc.gpsimd.affine_select(out=mask[:], in_=mask[:], compare_op=ALU.is_ge, fill=NEG, base=0,
                                         pattern=[[0, 4], [-1, P]], channel_multiplier=1))
            link(nc.gpsimd.memset(pick[:], 0.0))
            link(nc.gpsimd.affine_select(out=pick[:], in_=pick[:], compare_op=ALU.not_equal, fill=1.0, base=0,
                                         pattern=[[-1, NB], [0, P]], channel_multiplier=1))
            link(nc.gpsimd.memset(keep[:], 1.0))
            for j in range(0, NCH + 2, CPB):
                link(nc.gpsimd.memset(keep[:, j, :], 0.0))
            link(nc.gpsimd.memset(half[:], -0.5))
            link(nc.gpsimd.memset(hT[:, 1, :, :, CH:CH + 1].bitcast(F32), 0.0))
            link(nc.gpsimd.iota(iota[:], pattern=[[1, E]], base=0, channel_multiplier=0,
                                allow_small_or_imprecise_dtypes=True))
            assert chain.now() == N_CONST

            def rstd(j):
                pool.wait_ge(var_ready, j + 1)
                nc.gpsimd.tensor_tensor(rs[:, 1, :], rs[:, 0, :], half[:], ALU.pow).then_inc(rstd_ready, 1)

            def low_and_halo(j, slot, other):
                pool.wait_ge(h_hi, j + 1)
                nc.gpsimd.tensor_tensor(hT[:, bass.ds(slot, 1), LO, :, 1:CH + 1], hf[:].unsqueeze(1),
                                        hT[:, bass.ds(slot, 1), HI, :, 1:CH + 1].bitcast(F32),
                                        ALU.subtract).then_inc(h_ready, 1)
                pool.wait_ge(h_ready, 3 * j + 1)
                both = lambda s, col: hT[:, bass.ds(s, 1), :, :, col:col + 1].rearrange("p a b c d -> p (a b c) d")
                kj = keep[:, bass.ds(j, 1), :].rearrange("p a (b c) -> p (a b) c", c=1)
                nc.gpsimd.tensor_tensor(both(slot, 0), both(other, CH).bitcast(F32), kj, ALU.mult).then_inc(h_ready, 1)
                nc.gpsimd.tensor_tensor(both(other, CH + 1), both(slot, 1).bitcast(F32), kj, ALU.mult
                                        ).then_inc(h_ready, 1)

            for j in range(3):
                rstd(j)
                low_and_halo(j, j % 2, (j + 1) % 2)
            with pool.Fori(0, NCH - 1) as t:
                slot, other = pool.snap((t + 3) % 2), pool.snap(t % 2)
                pool.wait_ge(ld["xr"], 16 * t + 16)
                pool.wait_ge(m_done, N_MOD)
                for b in range(2):
                    nc.gpsimd.tensor_tensor(xr[:, b:b + 1, :], xr[:, b:b + 1, :], gaPB[:, bass.ds(t // CPB, 1), :],
                                            ALU.add).then_inc(xr_biased, 1)
                rstd(t + 3)
                low_and_halo(t + 3, slot, other)
            pool.wait_ge(ld["xr"], 16 * NCH)
            for b in range(2):
                nc.gpsimd.tensor_tensor(xr[:, b, :], xr[:, b, :], gaPB[:, NB - 1, :], ALU.add).then_inc(xr_biased, 1)

            def rstd2(i):
                pool.wait_ge(var2_ready, i + 1)
                nc.gpsimd.tensor_tensor(rs[:, 1, 0:1], rs[:, 0, 0:1], half[:, 0:1], ALU.pow).then_inc(rstd2_ready, 1)

            def bias2(i, slot, b):
                pool.wait_ge(xn2_ready, i + 1)
                nc.gpsimd.tensor_tensor(x2[:, bass.ds(slot, 1), :], x2[:, bass.ds(slot, 1), :],
                                        gbBB[:, bass.ds(b, 1), :], ALU.add).then_inc(x2_biased, 1)

            def low2(i, p):
                pool.wait_ge(h2_hi, i + 1)
                nc.gpsimd.tensor_tensor(h2[:, p, LO], hf2[:, p], h2[:, p, HI].bitcast(F32), ALU.subtract
                                        ).then_inc(h2_ready, 1)

            pool.wait_ge(o_done, N_PREP)
            for i in range(2):
                rstd2(i)
                bias2(i, i, 0)
                low2(i, i)
            with pool.Fori(0, NBLK // 2) as it:
                batch = pool.snap(((2 * it + 2) % NBLK) // BPB)
                for p in range(2):
                    i = 2 * it + p
                    rstd2(i + 2)
                    bias2(i + 2, (i + 2) % 4, batch)
                    low2(i + 2, p)

        @block.scalar
        def _(act):
            act.wait_ge(ld["c"], 16 * NB)
            nc.scalar.activation(silT[:, 1], silT[:, 0], ACT.Exp, scale=-1.0).then_inc(sil_exp, 1)

            def split(n):
                dst, raw, scale, loaded = splits[n]
                act.wait_ge(loaded, 16)
                nc.scalar.activation(dst[:, HI], raw if n < N_SPLIT - 2 else raw[:], ACT.Copy, scale=scale
                                     ).then_inc(split_hi, 1)

            def high(j, slot):
                act.wait_ge(t_done, j_done(j))
                nc.scalar.activation(hT[:, bass.ds(slot, 1), HI, :, 1:CH + 1], hf[:].unsqueeze(1), ACT.Copy
                                     ).then_inc(h_hi, 1)

            def j_done(j):
                return 2 * j + 2 if type(j) is int and j < 3 else t_at(j - 3, T_N)

            def conv_hi(base, j, n):
                act.wait_ge(w_full, base + n + 1)
                nc.scalar.activation(cv[:, n, HI], WB[(base_parity + n) % 2][:, 0:CH], ACT.Identity,
                                     bias=cb[:, n:n + 1]).then_inc(cv_hi, 1)

            def qk_high(index, parity, g):
                act.wait_ge(w_full, index + 1)
                for a in range(2):
                    nc.scalar.activation(qk16[:, HI, 2 * g + a], WB[parity][:, a * CH:(a + 1) * CH], ACT.Identity,
                                         bias=bqk[:, 2 * g + a:2 * g + a + 1]).then_inc(qk_hi, 1)

            def v_high(index, parity, g):
                act.wait_ge(w_full, index + 1)
                nc.scalar.activation(v16[:, HI, g // 2, (g % 2) * 512:(g % 2) * 512 + 512], WB[parity][:], ACT.Copy
                                     ).then_inc(v_hi, 1)

            for n in range(TAPS):
                split(n)
            high(0, 0)
            for n in range(TAPS, N_SPLIT - 2):
                split(n)
            high(1, 1)
            for n in range(N_SPLIT - 2, N_SPLIT):
                split(n)
            base_parity = 0
            act.wait_ge(ld["small"], 16 * SMALL)
            act.wait_ge(split_lo, N_SPLIT + 1)
            for n in range(3):
                conv_hi(0, 0, n)
            for g in range(8):
                qk_high(3 + g, (3 + g) % 2, g)
            for g in range(4):
                v_high(11 + g, (11 + g) % 2, g)
            high(2, 0)

            base_parity = W0 % 2

            def attend(t, ahead):
                def exps(u):
                    for bank in range(2):
                        for i in range(4):
                            if i == 0:
                                act.wait_ge(nm_ready, 8 * t + 2 * u + bank + 1)
                            n = 4 * bank + i
                            ins = nc.scalar.activation(prob[:, u, n], S[2 * (u % 2) + bank][:, i * P:(i + 1) * P],
                                                       ACT.Exp, bias=nm[:, u, n:n + 1],
                                                       accum_out=rsum[:, u, n:n + 1])
                        ins.then_inc(s_done, 1)

                def pt_high(u):
                    for g in range(2):
                        k = T_PT + 2 * u + g
                        act.wait_ge(t_full, t_at(t, k) + 1)
                        nc.scalar.activation(pt16[:, u % 2, HI, 4 * g:4 * g + 4], TB[(T0 + k) % 2][:].rearrange(
                            "p (h q) -> p h q", h=4), ACT.Copy).then_inc(pt_hi, 1)

                def ot_high(b):
                    for g in range(2):
                        k = T_OT + 2 * b + g
                        act.wait_ge(t_full, t_at(t, k) + 1)
                        nc.scalar.activation(oT[:, HI, 4 * g:4 * g + 4, b * P:(b + 1) * P],
                                             TB[(T0 + k) % 2][:].rearrange("p (h q) -> p h q", h=4), ACT.Copy
                                             ).then_inc(ot_hi, 1)

                exps(0)
                exps(1)
                if ahead:
                    conv_hi(w_at(t, W_CONV), t + 1, 0)
                exps(2)
                if ahead:
                    conv_hi(w_at(t, W_CONV), t + 1, 1)
                exps(3)
                if ahead:
                    conv_hi(w_at(t, W_CONV), t + 1, 2)
                pt_high(0)
                for u in range(4):
                    if ahead:
                        for a in range(2):
                            k = W_QKPV + 3 * u + a
                            qk_high(w_at(t, k), (W0 + k) % 2, 2 * u + a)
                    if u < 3:
                        pt_high(u + 1)
                    if u == 2:
                        ot_high(0)
                for g in range(2):
                    if ahead:
                        v_high(w_at(t, W_V + g), (W0 + W_V + g) % 2, g)
                ot_high(1)
                for g in range(2, 4):
                    if ahead:
                        v_high(w_at(t, W_V + g), (W0 + W_V + g) % 2, g)
                k = w_wo(ahead)
                act.wait_ge(w_full, w_at(t, k) + 1)
                nc.scalar.activation(att[:, HI], WB[(W0 + k) % 2][:, 0:CH], ACT.Identity, bias=bofs[:]
                                     ).then_inc(att_hi, 1)
                if ahead:
                    high(t + 3, act.snap((t + 3) % 2))

            w_wo = lambda ahead: W_WO if ahead else W_QKPV + 4 - 3
            with act.Fori(0, NCH - 1) as t:
                attend(t, True)
            attend(NCH - 1, False)

            def prep_high(n, dst, bank):
                act.wait_ge(o_full, n + 1)
                nc.scalar.activation(dst, bank, ACT.Copy).then_inc(prep_hi, 1)

            for j in range(ER):
                prep_high(j, btw[:, HI, j], S[j % 2][:])
            for c in range(DC):
                prep_high(ER + c, bsw[:, HI, c], S[(ER + c) % 2][:])

            def h2_high(i, p):
                act.wait_ge(l_done, i + 1)
                nc.scalar.activation(h2[:, p, HI], hf2[:, p], ACT.Copy).then_inc(h2_hi, 1)

            def router_exp(i, p):
                act.wait_ge(ng_ready, i + 1)
                nc.scalar.activation(ex[:], WB[p][:, R:ARW], ACT.Exp, bias=ng[:], accum_out=zz[:, 1:2]
                                     ).then_inc(ex_done, 1)
                nc.scalar.activation(zz[:, 2:3], top[:, 1:2], ACT.Exp, bias=ng[:]).then_inc(ex_done, 1)

            def gt_high(i, p):
                for g in range(2):
                    act.wait_ge(g_full, 2 * i + g + 1)
                    nc.scalar.activation(gT[:, p, HI, 4 * g:4 * g + 4], TB[g][:].rearrange("p (c q) -> p c q", c=4),
                                         ACT.Copy).then_inc(gt_hi, 1)

            h2_high(0, 0)
            router_exp(0, 0)
            h2_high(1, 1)
            with act.Fori(0, NBLK // 2) as it:
                for p in range(2):
                    i = 2 * it + p
                    gt_high(i, p)
                    router_exp(i + 1, 1 - p)
                    h2_high(i + 2, p)

        @block.vector
        def _(dve):
            chain = Tally(dve_chain)

            def link(instruction):
                chain.inc(instruction)
                dve.wait_ge(dve_chain, chain.now())

            def newton(n):
                link(nc.vector.tensor_tensor(rs[:, 2, 0:n], rs[:, 1, 0:n], rs[:, 1, 0:n], ALU.mult))
                link(nc.vector.tensor_tensor(rs[:, 3, 0:n], rs[:, 2, 0:n], rs[:, 0, 0:n], ALU.mult))
                link(nc.vector.tensor_scalar(rs[:, 2, 0:n], rs[:, 3, 0:n], -0.5, 1.5, ALU.mult, ALU.add))
                link(nc.vector.tensor_tensor(rs[:, 4, 0:n], rs[:, 2, 0:n], rs[:, 1, 0:n], ALU.mult))

            def norm_a(j):
                dve.wait_ge(ld["x"], 16 * (j + 1))
                for b in range(2):
                    ins = nc.vector.bn_stats(st[:, b], xln[:, b])
                link(ins)
                nc.vector.memset(rs[:, 3, 0:1], 0.0)
                for b in range(2):
                    ins = nc.vector.bn_aggr(mv[:, b], st[:, b])
                link(ins)
                nc.vector.tensor_scalar(rs[:, 0, :], mv[:, :, 1], EPS, None, ALU.add).then_inc(var_ready, 1)

            def norm_b(j):
                dve.wait_ge(rstd_ready, j + 1)
                newton(2)
                if not (type(j) is int and j == 0):
                    dve.wait_ge(t_full, 2 * j if type(j) is int and j < 4 else t_at(j - 4, T_N))
                for b in range(2):
                    nc.vector.tensor_scalar(xn[:, b], xln[:, b], mv[:, b, 0:1], rs[:, 4, b:b + 1],
                                            ALU.subtract, ALU.mult).then_inc(xn_ready, 1)

            N_NORM = 6

            def modulate(j, index, parity, batch):
                if not (type(j) is int and j == 0):
                    dve.wait_ge(h_ready, 3 * j)
                for g in range(2):
                    dve.wait_ge(t_full, index + g + 1)
                    for c in range(2):
                        n = 2 * g + c
                        ins = nc.vector.tensor_scalar(
                            hf[:, n, :], TB[(parity + g) % 2][:, c * CH:(c + 1) * CH],
                            modT[:, 1, n, bass.ds(batch, 1)], modT[:, 0, n, bass.ds(batch, 1)],
                            ALU.mult, ALU.add)
                    ins.then_inc(t_done, 1)

            def split_low(n):
                dst, raw, scale, _ = splits[n]
                dve.wait_ge(split_hi, n + 1)
                r = raw if n < N_SPLIT - 2 else raw[:]
                nc.vector.scalar_tensor_tensor(out=dst[:, LO], in0=r, scalar=scale, in1=dst[:, HI].bitcast(F32),
                                               op0=ALU.mult, op1=ALU.subtract).then_inc(split_lo, 1)

            def conv_lo(index, parity, j, n):
                dve.wait_ge(cv_hi, 3 * j + n + 1)
                nc.vector.scalar_tensor_tensor(out=cv[:, n, LO], in0=WB[parity][:, 0:CH], scalar=cb[:, n:n + 1],
                                               in1=cv[:, n, HI].bitcast(F32), op0=ALU.add, op1=ALU.subtract
                                               ).then_inc(w_done, 1)

            def qk_low(parity, j, g):
                dve.wait_ge(qk_hi, 16 * j + 2 * g + 2)
                for a in range(2):
                    c = 2 * g + a
                    ins = nc.vector.scalar_tensor_tensor(out=qk16[:, LO, c], in0=WB[parity][:, a * CH:(a + 1) * CH],
                                                         scalar=bqk[:, c:c + 1], in1=qk16[:, HI, c],
                                                         op0=ALU.add, op1=ALU.subtract)
                ins.then_inc(w_done, 1)

            def v_low(parity, j, g):
                dve.wait_ge(v_hi, 4 * j + g + 1)
                cols = slice((g % 2) * 512, (g % 2) * 512 + 512)
                nc.vector.tensor_tensor(v16[:, LO, g // 2, cols], WB[parity][:], v16[:, HI, g // 2, cols],
                                        ALU.subtract).then_inc(w_done, 1)

            norm_a(0)
            dve.wait_ge(sil_exp, 1)
            link(nc.vector.tensor_scalar(silT[:, 2], silT[:, 1], 1.0, None, ALU.add))
            link(nc.vector.reciprocal(silT[:, 1], silT[:, 2]))
            nc.vector.tensor_tensor(silT[:, 3], silT[:, 0], silT[:, 1], ALU.mult).then_inc(sil_done, 1)
            norm_b(0)
            order = [0, 1, 2, 3, 4, 5]
            for m in order[:2]:
                dve.wait_ge(m_full, m + 1)
                nc.vector.tensor_copy(mrow[m], S[m % 4][0:NB, :]).then_inc(m_done, 1)
            norm_a(1)
            dve.wait_ge(m_full, 3)
            link(nc.vector.tensor_copy(modT[:, 0:2], S[2][:, 0:2 * DC * NB].rearrange("p (m k b) -> p m k b", m=2, k=DC)))
            nc.vector.tensor_scalar(modT[:, 1], modT[:, 1], 1.0, None, ALU.add).then_inc(m_done, 1)
            dve.wait_ge(m_done, 3)
            modulate(0, 0, 0, 0)
            norm_b(1)
            for n in range(TAPS):
                split_low(n)
            modulate(1, 2, 0, 0)
            for n in range(TAPS, N_SPLIT - 2):
                split_low(n)
            dve.wait_ge(ld["small"], 16 * SMALL)
            for n in range(N_SPLIT - 2, N_SPLIT):
                split_low(n)
            nc.vector.tensor_scalar(bqk[:, 0:NC], bqk[:, 0:NC], DH ** -0.5, None, ALU.mult).then_inc(split_lo, 1)
            norm_a(2)
            for n in range(3):
                conv_lo(n, n % 2, 0, n)
            for g in range(8):
                qk_low((3 + g) % 2, 0, g)
            for g in range(4):
                v_low((11 + g) % 2, 0, g)
            norm_b(2)
            for m in order[2:]:
                dve.wait_ge(m_full, m + 2)
                ins = nc.vector.tensor_copy(mrow[m], S[(m + 1) % 4][0:NB, :])
                if m in (2, 5):
                    link(ins)
                    g, a, s = mrow[m], tmprow[:, 0], tmprow[:, 1]
                    link(nc.vector.scalar_tensor_tensor(out=a, in0=g, scalar=-1.0, in1=g, op0=ALU.mult, op1=ALU.max))
                    link(nc.vector.tensor_scalar(s, g, 0.0, 2.0, ALU.is_ge, ALU.mult))
                    link(nc.vector.tensor_scalar(a, a, 0.25, None, ALU.max))
                    ins = nc.vector.scalar_tensor_tensor(out=g, in0=s, scalar=-1.0, in1=a,
                                                         op0=ALU.add, op1=ALU.mult)
                ins.then_inc(m_done, 1)
            dve.wait_ge(m_full, 8)
            link(nc.vector.tensor_copy(modT[:, 2:4], S[3][:, 0:2 * DC * NB].rearrange("p (m k b) -> p m k b", m=2, k=DC)))
            nc.vector.tensor_scalar(modT[:, 3], modT[:, 3], 1.0, None, ALU.add).then_inc(m_done, 1)
            for b in range(NB):
                dve.wait_ge(m_full, 9 + b)
                nc.vector.tensor_copy(gaB[:, b], S[b][:]).then_inc(m_done, 1)
            dve.wait_ge(m_done, 8 + NB)
            dve.wait_ge(m_full, 11)
            for b in range(NB):
                nc.vector.tensor_tensor(gaPB[:, b], S[2][:], gaB[:, b], ALU.mult).then_inc(m_done, 1)
            dve.wait_ge(m_full, 12)
            nc.vector.tensor_scalar(bofs[:], S[3][:, 0:1], boT[:], None, ALU.add).then_inc(m_done, 1)
            modulate(2, 4, 0, 0)
            CHAIN0 = chain.now()

            def attend(t, ahead):
                chain.at(CHAIN0 + N_NORM * t)

                def maxima(u):
                    for bank in range(2):
                        dve.wait_ge(s_full, 8 * t + 2 * u + bank + 1)
                        nc.vector.tensor_reduce(nm[:, u, 4 * bank:4 * bank + 4],
                                                S[2 * (u % 2) + bank][:].rearrange("p (h k) -> p h k", h=4),
                                                AX.X, ALU.max, negate=True).then_inc(nm_ready, 1)

                def pt_low(u):
                    for g in range(2):
                        k = T_PT + 2 * u + g
                        dve.wait_ge(pt_hi, 8 * t + 2 * u + g + 1)
                        nc.vector.tensor_tensor(pt16[:, u % 2, LO, 4 * g:4 * g + 4],
                                                TB[(T0 + k) % 2][:].rearrange("p (h q) -> p h q", h=4),
                                                pt16[:, u % 2, HI, 4 * g:4 * g + 4], ALU.subtract
                                                ).then_inc(t_done, 1)

                def ot_low(b):
                    for g in range(2):
                        k = T_OT + 2 * b + g
                        dve.wait_ge(ot_hi, 4 * t + 2 * b + g + 1)
                        part = oT[:, :, 4 * g:4 * g + 4, b * P:(b + 1) * P]
                        nc.vector.tensor_tensor(part[:, LO], TB[(T0 + k) % 2][:].rearrange("p (h q) -> p h q", h=4),
                                                part[:, HI].bitcast(F32), ALU.subtract).then_inc(t_done, 1)

                def normalise(u):
                    b, hf_ = u // 2, u % 2
                    k = W_QKPV + 3 * u + 2 if ahead else u
                    dve.wait_ge(w_full, w_at(t, k) + 1)
                    v = lambda ap: ap.rearrange("p (c two e) -> p c two e", two=2, e=DH)
                    r = rinv[:, u, :].rearrange("p (two c) -> p c two", two=2).unsqueeze(3)
                    nc.vector.tensor_tensor(v(o[:, b, hf_ * 512:hf_ * 512 + 512]), v(WB[(W0 + k) % 2][:]),
                                            r.broadcast_to([P, 4, 2, DH]), ALU.mult).then_inc(w_done, 1)

                cpar = lambda n: (W0 + W_CONV + n) % 2
                maxima(0)
                maxima(1)
                if ahead:
                    conv_lo(0, cpar(0), t + 1, 0)
                maxima(2)
                if ahead:
                    conv_lo(0, cpar(1), t + 1, 1)
                maxima(3)
                if ahead:
                    norm_a(t + 3)
                    conv_lo(0, cpar(2), t + 1, 2)
                dve.wait_ge(s_done, 8 * t + 8)
                nc.vector.reciprocal(rinv[:], rsum[:]).then_inc(dve_chain, 1)
                chain.k += 1
                dve.wait_ge(dve_chain, chain.now())
                pt_low(0)
                for u in range(4):
                    if ahead:
                        for a in range(2):
                            k = W_QKPV + 3 * u + a
                            qk_low((W0 + k) % 2, t + 1, 2 * u + a)
                    if u < 3:
                        pt_low(u + 1)
                    normalise(u)
                    if u == 2:
                        ot_low(0)
                for g in range(2):
                    if ahead:
                        v_low((W0 + W_V + g) % 2, t + 1, g)
                ot_low(1)
                for g in range(2, 4):
                    if ahead:
                        v_low((W0 + W_V + g) % 2, t + 1, g)
                if ahead:
                    norm_b(t + 3)
                k = W_WO if ahead else 4
                dve.wait_ge(att_hi, t + 1)
                nc.vector.scalar_tensor_tensor(out=att[:, LO], in0=WB[(W0 + k) % 2][:, 0:CH], scalar=bofs[:],
                                               in1=att[:, HI].bitcast(F32), op0=ALU.add, op1=ALU.subtract
                                               ).then_inc(w_done, 1)
                if ahead:
                    modulate(t + 3, t_at(t, T_LN), (T0 + T_LN) % 2, dve.snap(((t + 3) % NCH) // CPB))
                batch = dve.snap(t // CPB) if ahead else NB - 1
                dve.wait_ge(xr_biased, 2 * t + 2)
                for b in range(2):
                    kk = k + 1 + b
                    dve.wait_ge(w_full, w_at(t, kk) + 1)
                    nc.vector.tensor_tensor(x1[:, b:b + 1, :], WB[(W0 + kk) % 2][:].unsqueeze(1),
                                            gaB[:, bass.ds(batch, 1), :], ALU.mult).then_inc(w_done, 1)
                    dve.wait_ge(w_done, w_at(t, kk) + 1)
                    nc.vector.tensor_tensor(x1[:, b], x1[:, b], xr[:, b], ALU.add).then_inc(x1_ready, 1)

            N_NORM = 6 + 1
            with dve.Fori(0, NCH - 1) as t:
                attend(t, True)
                assert chain.k == N_NORM, chain.k
            attend(NCH - 1, False)
            chain.at(CHAIN0 + N_NORM * (NCH - 1) + chain.k)

            for j in range(ER):
                dve.wait_ge(prep_hi, j + 1)
                nc.vector.tensor_tensor(btw[:, LO, j], S[j % 2][:], btw[:, HI, j].bitcast(F32), ALU.subtract
                                        ).then_inc(o_done, 1)
            for c in range(DC):
                dve.wait_ge(prep_hi, ER + c + 1)
                nc.vector.tensor_tensor(bsw[:, LO, c], S[(ER + c) % 2][:], bsw[:, HI, c].bitcast(F32), ALU.subtract
                                        ).then_inc(o_done, 1)
            n = ER + DC
            dve.wait_ge(o_full, n + 1)
            nc.vector.tensor_copy(arT[:], S[n % 2][:, 0:DC * ARW].rearrange("p (c a) -> p c a", c=DC)).then_inc(o_done, 1)
            n += 1
            for b in range(NB):
                dve.wait_ge(o_full, n + 1)
                nc.vector.tensor_copy(gbB[:, b], S[n % 2][:]).then_inc(o_done, 1)
                n += 1
                dve.wait_ge(o_done, n)
                dve.wait_ge(o_full, n + 1)
                nc.vector.tensor_tensor(gbBB[:, b], S[n % 2][:], gbB[:, b], ALU.mult).then_inc(o_done, 1)
                n += 1
            assert n == N_PREP

            def norm2(i, slot, loads, lsem):
                dve.wait_ge(lsem, loads)
                xi = x2[:, bass.ds(slot, 1), :]
                link(nc.vector.bn_stats(st[:, 0], xi.rearrange("p a d -> p (a d)")))
                nc.vector.memset(rs[:, 3, 0:1], 0.0)
                link(nc.vector.bn_aggr(mv[:, 0], st[:, 0]))
                nc.vector.tensor_scalar(rs[:, 0, 0:1], mv[:, 0, 1:2], EPS, None, ALU.add).then_inc(var2_ready, 1)
                dve.wait_ge(rstd2_ready, i + 1)
                newton(1)
                nc.vector.tensor_scalar(xn2[:].unsqueeze(1), xi, mv[:, 0, 0:1], rs[:, 4, 0:1],
                                        ALU.subtract, ALU.mult).then_inc(xn2_ready, 1)

            def modulate2(i, p, batch):
                dve.wait_ge(l_full, i + 1)
                for c in range(DC):
                    ins = nc.vector.tensor_scalar(hf2[:, p, c], S[2 + p][:, c * P:(c + 1) * P],
                                                  modT[:, 3, c, bass.ds(batch, 1)], modT[:, 2, c, bass.ds(batch, 1)],
                                                  ALU.mult, ALU.add)
                ins.then_inc(l_done, 1)

            def router(i, p):
                dve.wait_ge(a_full, i + 1)
                logits = WB[p][:, R:ARW]
                nc.vector.tensor_copy(res[:], WB[p][:, 0:R])
                link(nc.vector.max(top[:], logits))
                nc.vector.tensor_scalar(ng[:], top[:, 0:1], -1.0, None, ALU.mult).then_inc(ng_ready, 1)
                dve.wait_ge(ex_done, 2 * i + 2)
                nc.vector.tensor_scalar(zz[:, 3:4], zz[:, 1:2], 1e-6, 1.0, ALU.mult, ALU.add).then_inc(dve_chain, 1)
                nc.vector.max_index(topi[:], top[:], logits).then_inc(a_done, 1)
                chain.k += 1
                dve.wait_ge(dve_chain, chain.now())
                dve.wait_ge(a_done, i + 1)
                link(nc.vector.tensor_tensor(zz[:, 4:5], zz[:, 3:4], zz[:, 2:3], ALU.add))
                nc.vector.tensor_copy(topf[:], topi[:, 0:2]).then_inc(dve_chain, 1)
                chain.k += 1
                link(nc.vector.reciprocal(zz[:, 5:6], zz[:, 4:5]))
                link(nc.vector.tensor_scalar(zz[:, 6:7], zz[:, 5:6], 0.5, None, ALU.mult))
                link(nc.vector.tensor_scalar(cmb[:, 0], iota[:], topf[:, 0:1], zz[:, 6:7], ALU.is_equal, ALU.mult))
                link(nc.vector.tensor_tensor(zz[:, 7:8], zz[:, 6:7], zz[:, 2:3], ALU.mult))
                link(nc.vector.tensor_scalar(cmb[:, 1], iota[:], topf[:, 1:2], zz[:, 7:8], ALU.is_equal, ALU.mult))
                link(nc.vector.tensor_tensor(cmb[:, 0], cmb[:, 0], cmb[:, 1], ALU.add))
                nc.vector.tensor_tensor(G[:], cmb[:, 0].unsqueeze(2).broadcast_to([P, E, R]),
                                        res[:].unsqueeze(1).broadcast_to([P, E, R]), ALU.mult).then_inc(g_ready, 1)

            def gt_low(i, p):
                for g in range(2):
                    dve.wait_ge(gt_hi, 2 * i + g + 1)
                    nc.vector.tensor_tensor(gT[:, p, LO, 4 * g:4 * g + 4], TB[g][:].rearrange("p (c q) -> p c q", c=4),
                                            gT[:, p, HI, 4 * g:4 * g + 4].bitcast(F32), ALU.subtract
                                            ).then_inc(g_done, 1)

            norm2(0, 0, 16, ld_x2[0])
            modulate2(0, 0, 0)
            router(0, 0)
            norm2(1, 1, 16, ld_x2[1])
            modulate2(1, 1, 0)
            CHAIN2 = chain.now()
            N_BLK = 2 + 4 + 10
            with dve.Fori(0, NBLK // 4) as it:
                for q in range(4):
                    i, p = 4 * it + q, q % 2
                    chain.at(CHAIN2 + N_BLK * i)
                    gt_low(i, p)
                    norm2(i + 2, (q + 2) % 4, 16 * (it + (2 if q >= 2 else 1)), ld_x2[(q + 2) % 4])
                    router(i + 1, 1 - p)
                    modulate2(i + 2, p, dve.snap(((i + 2) % NBLK) // BPB))
                    dve.wait_ge(o_full, N_PREP + i + 1)
                    nc.vector.tensor_tensor(ob[:, p:p + 1, :], S[p][:].unsqueeze(1),
                                            gbB[:, bass.ds(dve.snap(i // BPB), 1), :], ALU.mult).then_inc(o_done, 1)
                    dve.wait_ge(o_done, N_PREP + i + 1)
                    dve.wait_ge(x2_biased, i + 1)
                    nc.vector.tensor_tensor(ob[:, p], ob[:, p], x2[:, q], ALU.add).then_inc(ob_ready, 1)
                    assert chain.k == N_BLK, chain.k

        @block.tensor
        def _(pe):
            def passes(dst, stat, mov, first=True, last=True):
                for n, (a, b) in enumerate(PASSES):
                    ins = nc.tensor.matmul(dst, stat(a), mov(b), start=first and n == 0, stop=last and n == 2)
                return ins

            def conv_steps(slot, index, parity):
                for n in range(3):
                    dst = WB[(parity + n) % 2][:, 0:CH]
                    for tap in range(TAPS):
                        for c in range(DC):
                            for k, (a, b) in enumerate(PASSES):
                                start, stop = tap + c + k == 0, tap == TAPS - 1 and c == DC - 1 and k == 2
                                if start and not (type(index) is int and index + n < 2):
                                    pe.wait_ge(w_done, index + n - 1)
                                ins = nc.tensor.matmul(
                                    dst, cw[:, a, tap, c, n * P:(n + 1) * P],
                                    hT[:, bass.ds(slot, 1), b, c, tap:tap + CH].rearrange("p a t -> p (a t)"),
                                    start=start, stop=stop)
                                if stop:
                                    ins.then_inc(w_full, 1)
                                yield

            def run(steps, n):
                for _ in range(n):
                    next(steps)

            def project_qk(index, parity, g, conv_done):
                pe.wait_ge(w_done, index - 1)
                pe.wait_ge(w_done, conv_done)
                for a in range(2):
                    c = 2 * g + a
                    n = c // NC
                    ins = passes(WB[parity][:, a * CH:(a + 1) * CH],
                                 lambda s: pw[:, s, n, (c % NC) * P:(c % NC + 1) * P], lambda m: cv[:, n, m])
                ins.then_inc(w_full, 1)

            def project_v(index, parity, g):
                pe.wait_ge(w_done, index - 1)
                ins = passes(WB[parity][:], lambda s: cv[:, 2, s, (g // 2) * P:(g // 2 + 1) * P],
                             lambda m: pw[:, m, 2, (g % 2) * 512:(g % 2) * 512 + 512])
                ins.then_inc(w_full, 1)

            def transpose_chunk(j, index, parity):
                pe.wait_ge(xn_ready, 2 * j + 2)
                for g in range(2):
                    if not (type(index) is int and index + g < 2):
                        pe.wait_ge(t_done, index + g - 1)
                    for c in range(2):
                        for b in range(2):
                            ins = nc.tensor.transpose(TB[(parity + g) % 2][:, c * CH + b * P:c * CH + (b + 1) * P],
                                                      xn[:, b, (2 * g + c) * P:(2 * g + c + 1) * P], ident[:])
                    ins.then_inc(t_full, 1)

            def mod_row(m, use):
                for k in range(DC):
                    ins = nc.tensor.matmul(S[use % 4][0:NB, :], silT[:, 3, k, :], wm[:, k, m, :],
                                           start=k == 0, stop=k == DC - 1)
                ins.then_inc(m_full, 1)

            def mod_columns(m, use):
                for i in range(2):
                    for k in range(DC):
                        at = (i * DC + k) * NB
                        ins = nc.tensor.transpose(S[use % 4][:, at:at + NB], mrow[m + i][:, k * P:(k + 1) * P],
                                                  ident[0:NB, 0:NB])
                ins.then_inc(m_full, 1)

            pe.wait_ge(pool_chain, N_CONST)
            transpose_chunk(0, 0, 0)
            pe.wait_ge(sil_done, 1)
            pe.wait_ge(ld["wm0"], 16)
            mod_row(0, 0)
            mod_row(1, 1)
            pe.wait_ge(m_done, 2)
            mod_columns(0, 2)
            transpose_chunk(1, 2, 0)
            pe.wait_ge(split_lo, TAPS)
            pe.wait_ge(h_ready, 6)
            steps = conv_steps(0, 0, 0)
            run(steps, 3 * TAPS * DC * 3)
            pe.wait_ge(split_lo, N_SPLIT)
            for g in range(8):
                project_qk(3 + g, (3 + g) % 2, g, 1 + g // 4)
            pe.wait_ge(w_done, 3)
            for g in range(4):
                project_v(11 + g, (11 + g) % 2, g)
            transpose_chunk(2, 4, 0)
            pe.wait_ge(ld["wm1"], 16)
            for m in range(2, 6):
                pe.wait_ge(m_done, m - 2)
                mod_row(m, m + 1)
            pe.wait_ge(m_done, 7)
            mod_columns(3, 7)
            for b in range(NB):
                nc.tensor.matmul(S[b][:], pick[:, b, :], mrow[2], start=True, stop=True).then_inc(m_full, 1)
            pe.wait_ge(ld["small"], 16 * SMALL)
            nc.tensor.matmul(S[2][:], pick[0:1, 0, :], brow[:], start=True, stop=True).then_inc(m_full, 1)
            pe.wait_ge(m_done, 8)
            for c in range(NC):
                for a in range(2):
                    ins = nc.tensor.matmul(S[3][:, 0:1], wow[:, a, c, :].bitcast(F32), bvT[:, c:c + 1],
                                           start=c + a == 0, stop=c == NC - 1 and a == 1)
            ins.then_inc(m_full, 1)
            pe.wait_ge(m_done, N_MOD)

            def attend(t, ahead):
                def scores(u):
                    b, half_ = u // 2, u % 2
                    use = 8 * t + 2 * u
                    if u >= 2:
                        pe.wait_ge(s_done, use - 2)
                    elif ahead:
                        pe.wait_ge(w_done, w_at(t, 0))
                    for bank in range(2):
                        nc.tensor.matmul(S[2 * (u % 2) + bank][:], ident16[:], mask[:].rearrange("p h k -> p (h k)"),
                                         start=True, stop=False)
                    for i in range(4):
                        c = 4 * half_ + i
                        for n, (a, m) in enumerate(PASSES):
                            for bank in range(2):
                                rows = slice(DH * bank, DH * (bank + 1))
                                ins = nc.tensor.matmul(S[2 * (u % 2) + bank][:, i * P:(i + 1) * P],
                                                       qk16[rows, a, c, b * P:(b + 1) * P],
                                                       qk16[rows, m, NC + c, b * P:(b + 1) * P],
                                                       start=False, stop=i == 3 and n == 2)
                                if i == 3 and n == 2:
                                    ins.then_inc(s_full, 1)

                def transpose_p(u):
                    pe.wait_ge(s_done, 8 * t + 2 * u + 2)
                    for g in range(2):
                        k = T_PT + 2 * u + g
                        pe.wait_ge(t_done, t_at(t, k) - 1)
                        for i in range(4):
                            ins = nc.tensor.transpose(TB[(T0 + k) % 2][:, i * P:(i + 1) * P],
                                                      prob[:, u, 4 * g + i, :], ident[:])
                        ins.then_inc(t_full, 1)

                def pv(u):
                    b, half_ = u // 2, u % 2
                    k = W_QKPV + 3 * u + 2 if ahead else u
                    pe.wait_ge(w_done, w_at(t, k) - 1)
                    pe.wait_ge(t_done, t_at(t, T_PT + 2 * u + 2))
                    for n in range(8):
                        head = 2 * (n % 4) + n // 4
                        ins = passes(WB[(W0 + k) % 2][:, head * DH:(head + 1) * DH],
                                     lambda s: pt16[:, u % 2, s, n, :],
                                     lambda m: v16[:, m, b, (8 * half_ + head) * DH:(8 * half_ + head + 1) * DH])
                    ins.then_inc(w_full, 1)

                def transpose_o(b):
                    kk = W_QKPV + 3 * (2 * b + 1) + 2 if ahead else 2 * b + 1
                    pe.wait_ge(w_done, w_at(t, kk) + 1)
                    for g in range(2):
                        k = T_OT + 2 * b + g
                        pe.wait_ge(t_done, t_at(t, k) - 1)
                        for i in range(4):
                            c = 4 * g + i
                            ins = nc.tensor.transpose(TB[(T0 + k) % 2][:, i * P:(i + 1) * P],
                                                      o[:, b, c * P:(c + 1) * P], ident[:])
                        ins.then_inc(t_full, 1)

                if ahead:
                    pe.wait_ge(h_ready, 3 * t + 9)
                    steps = conv_steps(pe.snap((t + 1) % 2), w_at(t, W_CONV), (W0 + W_CONV) % 2)
                    part = 3 * TAPS * DC * 3 // 4
                for u in range(4):
                    scores(u)
                    if ahead:
                        run(steps, part)
                transpose_p(0)
                for u in range(4):
                    if ahead:
                        for a in range(2):
                            k = W_QKPV + 3 * u + a
                            g = 2 * u + a
                            project_qk(w_at(t, k), (W0 + k) % 2, g, w_at(t, W_CONV + 1 + g // 4))
                    if u < 3:
                        transpose_p(u + 1)
                    pv(u)
                    if u == 2:
                        transpose_o(0)
                for g in range(2):
                    if ahead:
                        project_v(w_at(t, W_V + g), (W0 + W_V + g) % 2, g)
                transpose_o(1)
                for g in range(2, 4):
                    if ahead:
                        project_v(w_at(t, W_V + g), (W0 + W_V + g) % 2, g)
                k = W_WO if ahead else 4
                pe.wait_ge(w_done, w_at(t, k) - 1)
                pe.wait_ge(t_done, t_at(t, T_OT + 4))
                for c in range(NC):
                    ins = passes(WB[(W0 + k) % 2][:, 0:CH], lambda s: wow[:, s, c, :], lambda m: oT[:, m, c, :],
                                 c == 0, c == NC - 1)
                ins.then_inc(w_full, 1)
                if ahead:
                    transpose_chunk(t + 3, t_at(t, T_LN), (T0 + T_LN) % 2)
                pe.wait_ge(w_done, w_at(t, k) + 1)
                for b in range(2):
                    if b == 1:
                        pe.wait_ge(w_done, w_at(t, k + 1 + b) - 1)
                    ins = passes(WB[(W0 + k + 1 + b) % 2][:], lambda s: att[:, s, b * P:(b + 1) * P],
                                 lambda m: pjw[:, m, :])
                    ins.then_inc(w_full, 1)

            with pe.Fori(0, NCH - 1) as t:
                attend(t, True)
            attend(NCH - 1, False)

            pe.wait_ge(ld["raw"], 16 * (3 + DC))
            pe.wait_ge(w_done, w_at(NCH - 1, 7))
            for j in range(ER):
                if j >= 2:
                    pe.wait_ge(o_done, j - 1)
                for c in range(DC):
                    ins = nc.tensor.transpose(S[j % 2][:, c * P:(c + 1) * P],
                                              braw[:, c, 2 * j:2 * j + 2, :].rearrange("p e r -> p (e r)"), ident[:])
                ins.then_inc(o_full, 1)
            for i in range(DC):
                n = ER + i
                pe.wait_ge(o_done, n - 1)
                for c in range(DC):
                    ins = nc.tensor.transpose(S[n % 2][:, c * P:(c + 1) * P], bsraw[:, c, i * P:(i + 1) * P], ident[:])
                ins.then_inc(o_full, 1)
            n = ER + DC
            pe.wait_ge(o_done, n - 1)
            for c in range(DC):
                ins = nc.tensor.transpose(S[n % 2][:, c * ARW:(c + 1) * ARW], arraw[:, c * P:(c + 1) * P],
                                          ident[0:ARW, 0:ARW])
            ins.then_inc(o_full, 1)
            n += 1
            pe.wait_ge(ld["brow2"], 16)
            for b in range(NB):
                pe.wait_ge(o_done, n - 1)
                nc.tensor.matmul(S[n % 2][:], pick[:, b, :], gbrow[:], start=True, stop=True).then_inc(o_full, 1)
                n += 1
                pe.wait_ge(o_done, n - 1)
                nc.tensor.matmul(S[n % 2][:], pick[0:1, 0, :], brow2[:], start=True, stop=True).then_inc(o_full, 1)
                n += 1
            pe.wait_ge(o_done, n)

            def transpose_x2(i, p):
                pe.wait_ge(xn2_ready, i + 1)
                if not (type(i) is int and i < 2):
                    pe.wait_ge(l_done, i - 1)
                for c in range(DC):
                    ins = nc.tensor.transpose(S[2 + p][:, c * P:(c + 1) * P], xn2[:, c * P:(c + 1) * P], ident[:])
                ins.then_inc(l_full, 1)

            def low_rank(i, p):
                pe.wait_ge(l_done, i + 1)
                if not (type(i) is int and i == 0):
                    pe.wait_ge(a_done, i)
                for c in range(DC):
                    ins = nc.tensor.matmul(WB[p][:, 0:ARW], hf2[:, p, c, :], arT[:, c, :], start=c == 0, stop=c == DC - 1)
                ins.then_inc(a_full, 1)

            def transpose_g(i, p):
                pe.wait_ge(g_ready, i + 1)
                for g in range(2):
                    if not (type(i) is int and i == 0):
                        pe.wait_ge(g_done, 2 * i + g - 1)
                    for c in range(4):
                        k = 4 * g + c
                        ins = nc.tensor.transpose(TB[g][:, c * P:(c + 1) * P],
                                                  G[:, 2 * k:2 * k + 2, :].rearrange("p e r -> p (e r)"), ident[:])
                    ins.then_inc(g_full, 1)

            transpose_x2(0, 0)
            low_rank(0, 0)
            transpose_x2(1, 1)
            transpose_g(0, 0)
            with pe.Fori(0, NBLK // 2) as it:
                for p in range(2):
                    i = 2 * it + p
                    pe.wait_ge(h2_ready, i + 1)
                    pe.wait_ge(o_done, N_PREP + i - 1)
                    for c in range(DC):
                        passes(S[p][:], lambda s: h2[:, p, s, c, :], lambda m: bsw[:, m, c, :], c == 0, False)
                    low_rank(i + 1, 1 - p)
                    transpose_x2(i + 2, p)
                    pe.wait_ge(g_done, 2 * i + 2)
                    for c in range(ER):
                        ins = passes(S[p][:], lambda s: gT[:, p, s, c, :], lambda m: btw[:, m, c, :], False, c == ER - 1)
                    ins.then_inc(o_full, 1)
                    transpose_g(i + 1, 1 - p)


_INS = ['L0_attn_inputs', 'L0_attn_conv_w', 'L0_attn_conv_b', 'L0_attn_wq', 'L0_attn_bq', 'L0_attn_wk',
        'L0_attn_bk', 'L0_attn_wv', 'L0_attn_bv', 'L0_attn_wo', 'L0_attn_bo', 'L0_attn_proj_w',
        'L0_attn_proj_b', 'L0_ffn_base_w', 'L0_ffn_base_b', 'L0_ffn_A', 'L0_ffn_B', 'L0_ffn_router_w',
        'L0_c', 'L0_wmod']
_OUTS = [((2, 1024, 512), 'float32')]


def kernel(**inputs):
    import numpy as _np
    import concourse.bacc as _bacc
    from concourse import mybir as _mybir
    from concourse.bass_utils import run_bass_kernel_spmd as _run

    nc = _bacc.Bacc("TRN2", target_bir_lowering=False, num_devices=1)
    arrays, args = {}, []
    for name in _INS:
        a = _np.ascontiguousarray(inputs[name])
        arrays[f"in_{name}_dram"] = a
        args.append(nc.dram_tensor(f"in_{name}_dram", a.shape, _mybir.dt.from_np(a.dtype), kind="ExternalInput").ap())
    for i, (shape, dtype) in enumerate(_OUTS):
        dt = _mybir.dt.from_np(_np.dtype(dtype))
        args.append(nc.dram_tensor(f"out_{i}_dram", shape, dt, kind="ExternalOutput").ap())
    bass_adaln_block(nc, *args)
    r = _run(nc, [arrays], core_ids=[0])
    got = tuple(r.results[0][f"out_{i}_dram"] for i in range(len(_OUTS)))
    return got[0]
```

```python
from contextlib import ExitStack

import concourse.bass as bass
from concourse import mybir

ALU = mybir.AluOpType
ACT = mybir.ActivationFunctionType
AX = mybir.AxisListType
F32 = mybir.dt.float32
F32R = mybir.dt.float32r
F16 = mybir.dt.float16
BF16 = mybir.dt.bfloat16
U32 = mybir.dt.uint32

P = 128
EPS = 1e-5
NEG = -1e9
HI, LO = 0, 1
PASSES = [(HI, HI), (HI, LO), (LO, HI)]


class Tally:

    def __init__(self, sem):
        self.sem, self.before, self.k = sem, 0, 0

    def at(self, before):
        self.before, self.k = before, 0

    def inc(self, instruction):
        self.k += 1
        return instruction.then_inc(self.sem, 1)

    def now(self):
        return self.before + self.k


def bass_adaln_block(nc, x, conv_w, conv_b, wq, bq, wk, bk, wv, bv, wo, bo, proj_w, proj_b,
                     base_w, base_b, lora_a, lora_b, router_w, cond, wmod, out):
    NB, L, D = x.shape
    TAPS, _, C3 = conv_w.shape
    W = C3 // 3
    _, H, DH = wq.shape
    HE = H * DH
    E, _, R = lora_b.shape
    DC = D // P
    NC = HE // P
    CH = 2 * P
    NCH = NB * L // CH
    CPB = L // CH
    NBLK = NB * L // P
    BPB = L // P
    ER = E * R // P
    ARW = R + E
    assert W == P and D == 4 * P and 2 * DH == P and 2 * R == P

    CONV_N = 3 * TAPS * DC * 3
    STEP = [("s", 0), ("s", 1), ("c", 12), ("c", 12), ("pt", 0), ("c", 12), ("s", 2), ("pv", 0), ("c", 9),
            ("pt", 1), ("s", 3), ("na", 0), ("c", 9), ("pv", 1), ("c", 9), ("pt", 2), ("qk", 0), ("c", 9),
            ("qk", 1), ("pv", 2), ("ot", 0), ("c", 9), ("qk", 2), ("pt", 3), ("c", 9), ("qk", 3), ("c", 9),
            ("pv", 3), ("qk", 4), ("c", 9), ("qk", 5), ("ot", 1), ("qk", 6), ("nb", 0), ("v", 0), ("qk", 7),
            ("v", 1), ("wo", 0), ("ln", 0), ("v", 2), ("v", 3), ("pr", 0), ("pr", 1)]
    LAST = [("s", 0), ("s", 1), ("pt", 0), ("s", 2), ("pv", 0), ("pt", 1), ("s", 3), ("pv", 1), ("pt", 2),
            ("b", 0), ("b", 1), ("pv", 2), ("ot", 0), ("b", 2), ("b", 3), ("pt", 3), ("b", 4), ("b", 5),
            ("b", 6), ("pv", 3), ("b", 7), ("b", 8), ("b", 9), ("ot", 1), ("b", 10), ("b", 11), ("b", 12),
            ("wo", 0), ("b", 13), ("b", 14), ("na2", 0), ("b", 15), ("pr", 0),
            ("nb2", 0), ("b", 16), ("pr", 1)]
    STEP_ACT = [stage for stage in STEP if stage[0] != "ln"] + [("ln", 0)]
    assert sum(n for stage, n in STEP if stage == "c") == CONV_N

    def uses(order, cost):
        at, k = {}, 0
        for stage in order:
            if stage[0] in cost:
                at[stage] = k
                k += cost[stage[0]]
        return at, k

    W_USE, W_N = uses(STEP, {"pv": 1, "wo": 1, "pr": 1})
    W_N -= 1
    T_USE, T_N = uses(STEP, {"pt": 2, "ot": 2, "ln": 2})
    P_USE, P_N = uses(STEP, {"qk": 1, "v": 1})
    W_LAST, T_LAST = W_USE, uses(LAST, {"pt": 2, "ot": 2})[0]
    C_N, C_PR = 4, 3
    C0, P0 = 3, P_N
    W0 = 5
    T0 = 6
    assert T_N % 2 == 0 and P_N % 4 == 0 and W_USE["pr", 0] == W_N - 1

    xin = x.rearrange("n (c b p) d -> (n c) p b d", p=P, b=2)
    x1_chunk = out.rearrange("n (c b p) d -> (n c) p b d", p=P, b=2)
    x1_block = out.rearrange("n (b p) d -> (n b) p d", p=P)

    with ExitStack() as ctx:
        def sem(name):
            return ctx.enter_context(nc.semaphore(name))

        def psum(name, shape=(P, 512), dt=F32):
            return ctx.enter_context(nc.psum_tensor(name, list(shape), dt))

        slab = ctx.enter_context(nc.sbuf_tensor("slab", [P, 53200], F32))
        first = nc.sbuf_base - 4 * 53200
        place = [first]

        def put(name, shape, dt, at=None):
            size = {F32: 4, F32R: 4, F16: 2, BF16: 2, U32: 4}[dt]
            n = size
            for s in shape[1:]:
                n *= s
            where = place[0] if at is None else at
            t = nc.alloc_sbuf_tensor_at(name, list(shape), dt, offset=where)
            if at is None:
                place[0] += (n + 31) // 32 * 32
            return t, where

        cw, cw_at = put("cw", [P, 2, TAPS, DC, C3], F32R)
        pw, pw_at = put("pw", [P, 2, 3, HE], F32R)
        hT, _ = put("hT", [P, 2, 2, DC, CH + 2], F32R)
        f_end = place[0]
        wow, wow_at = put("wow", [P, 2, NC, W], F32R)
        pjw, pjw_at = put("pjw", [P, 2, D], F32R)
        common = place[0]
        cv, _ = put("cv", [P, 3, 2, CH], F32R)
        xln, xln_at = put("xln", [P, 2, D], F32)
        xn, _ = put("xn", [P, 2, D], F32)
        hf, _ = put("hf", [P, DC, CH], F32)
        qk16, qk16_at = put("qk16", [P, 2, 2 * NC, CH], F16)
        v16, _ = put("v16", [P, 2, 2, HE], F16)
        prob, prob_at = put("prob", [P, 4, 8, P], F32)
        pt16, _ = put("pt16", [P, 2, 2, 8, P], F16)
        o, _ = put("o", [P, 2, HE], F32)
        oT, _ = put("oT", [P, 2, NC, CH], F32R)
        att, _ = put("att", [P, 2, CH], F32R)
        xr, xr_at = put("xr", [P, 2, D], F32)
        x1, _ = put("x1", [P, 2, D], F32)
        gaB, _ = put("gaB", [P, NB, D], F32)
        gaPB, _ = put("gaPB", [P, NB, D], F32)
        ident, _ = put("ident", [P, P], F32)
        ident16, _ = put("ident16", [P, P], BF16)
        mask, _ = put("mask", [P, 4, P], BF16)
        modT, _ = put("modT", [P, 4, DC, NB], F32)
        gbrow, _ = put("gbrow", [NB, D], F32)
        pick, _ = put("pick", [NB, NB, P], F32)
        keep, _ = put("keep", [P, NCH + 2, 2 * DC], F32)
        half, _ = put("half", [P, 2], F32)
        cb, _ = put("cb", [P, 3], F32)
        bqk, _ = put("bqk", [P, 2 * NC], F32)
        bvT, _ = put("bvT", [P, NC], F32)
        boT, _ = put("boT", [P, 1], F32)
        bofs, _ = put("bofs", [P, 1], F32)
        silT, _ = put("silT", [P, 4, DC, NB], F32)
        st, _ = put("st", [P, 2, 6], F32)
        mv, _ = put("mv", [P, 2, 2], F32)
        rs, _ = put("rs", [P, 5, 2], F32)
        nm, _ = put("nm", [P, 4, 8], F32)
        rsum, _ = put("rsum", [P, 4, 8], F32)
        rinv, _ = put("rinv", [P, 4, 8], F32)
        iota, _ = put("iota", [P, E], F32)
        tmprow, tmprow_at = put("tmprow", [NB, 2, D], F32)
        assert place[0] <= nc.sbuf_base
        cw_raw, _ = put("cw_raw", [P, TAPS, DC, C3], F32, at=cw_at + 4 * TAPS * DC * C3)
        pw_raw, _ = put("pw_raw", [P, 3, HE], F32, at=pw_at + 4 * 3 * HE)
        wow_raw, _ = put("wow_raw", [P, NC, W], F32, at=wow_at + 4 * NC * W)
        pjw_raw, _ = put("pjw_raw", [P, D], F32, at=pjw_at + 4 * D)
        wm, _ = put("wm", [P, DC, 3, D], F32, at=prob_at)
        arow, _ = put("arow", [NB, 3, D], F32, at=xr_at)
        brow, _ = put("brow", [1, D], F32, at=xr_at + 4 * 3 * D)
        mrow = [arow[:, 0], arow[:, 1], arow[:, 2]]
        mrow2 = [arow[:, 0], arow[:, 1], gbrow[:]]
        brow2, _ = put("brow2", [1, D], F32, at=tmprow_at)
        place[0] = cw_at
        bsraw, _ = put("bsraw", [P, DC, D], F32)
        arraw, _ = put("arraw", [ARW, D], F32)
        braw, _ = put("braw", [P, DC, E, R], F32)
        btw, _ = put("btw", [P, 2, ER, D], F32R)
        bsw, _ = put("bsw", [P, 2, DC, D], F32R)
        arT, _ = put("arT", [P, DC, ARW], F32)
        assert place[0] <= f_end
        place[0] = common
        x2, _ = put("x2", [P, 4, D], F32)
        gbB, _ = put("gbB", [P, NB, D], F32)
        gbBB, _ = put("gbBB", [P, NB, D], F32)
        xn2, _ = put("xn2", [P, D], F32)
        assert place[0] <= qk16_at
        hf2, _ = put("hf2", [P, 2, DC, P], F32)
        h2, _ = put("h2", [P, 2, 2, DC, P], F32R)
        res, _ = put("res", [P, R], F32)
        G, _ = put("G", [P, E, R], F32)
        gT, _ = put("gT", [P, 2, 2, ER, P], F32R)
        ob, _ = put("ob", [P, 2, D], F32)
        top, _ = put("top", [P, 8], F32)
        topi, _ = put("topi", [P, 8], U32)
        topf, _ = put("topf", [P, 2], F32)
        ng, _ = put("ng", [P, 1], F32)
        ex, _ = put("ex", [P, E], F32)
        zz, _ = put("zz", [P, 8], F32)
        cmb, _ = put("cmb", [P, 2, E], F32)

        S = [psum(f"S{i}") for i in range(4)]
        CB = psum("CB")
        WB = psum("WB")
        TB = [psum(f"T{i}") for i in range(2)]
        AB = [WB, CB]

        dma_names = ["c", "xa", "wm0", "wm1", "wm2", "pq", "pk", "pv", "wo", "pj", "small", "x", "xr",
                     "ar", "braw", "raw", "x2a", "x2b", "x2c", "x2d", "brow2"]
        ld = {n: sem("ld_" + n) for n in dma_names}
        x1_stored, out_stored0, out_stored1 = sem("x1_stored"), sem("out_stored0"), sem("out_stored1")
        w_full, w_done, t_full, t_done, s_full, s_done = (
            sem(n) for n in ("w_full", "w_done", "t_full", "t_done", "s_full", "s_done"))
        c_full, c_done, p_full, p_done = (sem(n) for n in ("c_full", "c_done", "p_full", "p_done"))
        m_full, m_done = sem("m_full"), sem("m_done")
        sil_exp, sil_done, split_hi, split_lo = (
            sem(n) for n in ("sil_exp", "sil_done", "split_hi", "split_lo"))
        var_ready, rstd_ready, xn_ready, h_hi, h_ready = (
            sem(n) for n in ("var_ready", "rstd_ready", "xn_ready", "h_hi", "h_ready"))
        pool_chain, dve_chain = sem("pool_chain"), sem("dve_chain")
        cv_hi, qk_hi, v_hi, pt_hi, ot_hi, att_hi = (
            sem(n) for n in ("cv_hi", "qk_hi", "v_hi", "pt_hi", "ot_hi", "att_hi"))
        nm_ready, xr_biased, x1_ready = sem("nm_ready"), sem("xr_biased"), sem("x1_ready")
        o_full, o_done, a_full, a_done, l_full, l_done, g_full, g_done = (
            sem(n) for n in ("o_full", "o_done", "a_full", "a_done", "l_full", "l_done", "g_full", "g_done"))
        prep_hi, var2_ready, rstd2_ready, xn2_ready, h2_hi, h2_ready = (
            sem(n) for n in ("prep_hi", "var2_ready", "rstd2_ready", "xn2_ready", "h2_hi", "h2_ready"))
        x2_biased, ng_ready, ex_done, g_ready, gt_hi, ob_ready = (
            sem(n) for n in ("x2_biased", "ng_ready", "ex_done", "g_ready", "gt_hi", "ob_ready"))
        ld_x2 = [ld["x2a"], ld["x2b"], ld["x2c"], ld["x2d"]]
        out_stored = [out_stored0, out_stored1]
        ld_cw = [sem(f"ld_cw{i}") for i in range(TAPS)]

        w_at = lambda t, k: W0 + W_N * t + k
        t_at = lambda t, k: T0 + T_N * t + k
        c_at = lambda t, k: C0 + C_N * t + k
        c_pr = lambda t, ahead: c_at(t, C_PR if ahead else 0)
        p_at = lambda t, k: P0 + P_N * t + k
        N_MOD = 3 + 1 + NB + NB
        PREP_A, PREP_B = 2 * NB, 2 * NB + 1
        PREP_W, N_PREP = PREP_B + ER, PREP_B + ER + DC

        splits = [(cw[:, :, i], cw_raw[:, i], 1.0, ld_cw[i]) for i in range(TAPS)]
        splits += [(pw[:, :, 0], pw_raw[:, 0], DH ** -0.5, ld["pq"]), (pw[:, :, 1], pw_raw[:, 1], 1.0, ld["pk"]),
                   (pw[:, :, 2], pw_raw[:, 2], 1.0, ld["pv"]), (wow, wow_raw, 1.0, ld["wo"]),
                   (pjw, pjw_raw, 1.0, ld["pj"])]
        N_SPLIT = len(splits)
        N_CONST = 11 + len(range(0, NCH + 2, CPB))
        SMALL = 6

        block = ctx.enter_context(nc.Block())

        @block.sync
        def _(sp):
            sp.dma_start(xln[:], xin[0]).then_inc(ld["x"], 16)
            wmod_v = wmod.rearrange("(k p) (m d) -> p k m d", p=P, m=6)
            sp.dma_start(wm[:, :, 0:2, :], wmod_v[:, :, 0:2, :]).then_inc(ld["wm0"], 16)
            for i in range(TAPS):
                if i == 1:
                    sp.wait_ge(xn_ready, 2)
                    sp.dma_start(xln[:], xin[1]).then_inc(ld["x"], 16)
                sp.dma_start(cw_raw[:, i], conv_w[i].rearrange("(c p) o -> p c o", p=P)).then_inc(ld_cw[i], 16)
            for i, (w, name) in enumerate(((wq, "pq"), (wk, "pk"), (wv, "pv"))):
                sp.dma_start(pw_raw[:, i, :], w.rearrange("d h e -> d (h e)")).then_inc(ld[name], 16)
            sp.dma_start(wm[:, :, 2, :], wmod_v[:, :, 2, :]).then_inc(ld["wm1"], 16)
            sp.dma_start(wow_raw[:], wo.rearrange("h e d -> (h e) d").rearrange("(c p) d -> p c d", p=P)
                         ).then_inc(ld["wo"], 16)
            sp.dma_start(pjw_raw[:], proj_w).then_inc(ld["pj"], 16)
            sp.wait_ge(xn_ready, 4)
            sp.dma_start(xln[:], xin[2]).then_inc(ld["x"], 16)
            sp.wait_ge(m_full, 4)
            sp.dma_start(wm[:], wmod_v[:, :, 3:6, :]).then_inc(ld["wm2"], 16)
            sp.wait_ge(w_done, W0)
            sp.dma_start(brow2[:], base_b.rearrange("(a d) -> a d", a=1)).then_inc(ld["brow2"], 16)
            sp.wait_ge(m_done, N_MOD)
            sp.dma_start(xr[:], xin[0]).then_inc(ld["xr"], 16)

            with sp.Fori(0, NCH - 1) as t:
                sp.wait_ge(xn_ready, 2 * t + 6)
                sp.dma_start(xln[:], xin[bass.ds((t + 3) % NCH, 1)].rearrange("a p b d -> p (a b) d")
                             ).then_inc(ld["x"], 16)
                sp.wait_ge(x1_ready, 2 * t + 2)
                sp.dma_start(x1_chunk[bass.ds(t, 1)].rearrange("a p b d -> p (a b) d"), x1[:]
                             ).then_inc(x1_stored, 16)
                sp.wait_ge(x1_stored, 16 * t + 16)
                sp.dma_start(xr[:], xin[bass.ds(t + 1, 1)].rearrange("a p b d -> p (a b) d")
                             ).then_inc(ld["xr"], 16)
            sp.wait_ge(p_full, p_at(NCH - 2, P_N))
            sp.wait_ge(h_ready, 3 * (NCH + 2))
            sp.dma_start(arraw[0:R, :], lora_a).then_inc(ld["ar"], 16)
            sp.dma_start(arraw[R:ARW, :], router_w).then_inc(ld["ar"], 16)
            for c in range(DC):
                sp.dma_start(braw[:, c], lora_b[:, c * P:(c + 1) * P, :].rearrange("e p r -> p e r")
                             ).then_inc(ld["braw"], 16)
            sp.dma_start(bsraw[:], base_w.rearrange("(c p) i -> p c i", p=P)).then_inc(ld["raw"], 16)
            sp.wait_ge(x1_stored, 16 * (NCH - 1))
            for i in range(4):
                sp.dma_start(x2[:, i, :], x1_block[i]).then_inc(ld_x2[i], 16)
            sp.wait_ge(x1_ready, 2 * NCH)
            sp.dma_start(x1_chunk[NCH - 1], x1[:]).then_inc(x1_stored, 16)
            sp.wait_ge(x1_stored, 16 * NCH)
            with sp.Fori(0, NBLK // 4) as it:
                for q in range(4):
                    i = 4 * it + q
                    sp.wait_ge(ob_ready, i + 1)
                    sp.dma_start(x1_block[bass.ds(i, 1)].rearrange("a p d -> (a p) d"), ob[:, q % 2, :]
                                 ).then_inc(out_stored[q % 2], 16)
                    sp.wait_ge(out_stored[q % 2], 16 * (2 * it + q // 2 + 1))
                    sp.dma_start(x2[:, q, :], x1_block[bass.ds((i + 4) % NBLK, 1)].rearrange("a p d -> (a p) d")
                                 ).then_inc(ld_x2[q], 16)
            for q in range(4):
                sp.wait_ge(ld_x2[q], 16 * (NBLK // 4 + 1))

        @block.gpsimd
        def _(pool):
            chain = Tally(pool_chain)

            def link(instruction):
                chain.inc(instruction)
                pool.wait_ge(pool_chain, chain.now())

            def rstd(j):
                pool.wait_ge(var_ready, j + 1)
                nc.gpsimd.tensor_tensor(rs[:, 1, :], rs[:, 0, :], half[:], ALU.pow).then_inc(rstd_ready, 1)

            def low_and_halo(j, slot, other):
                pool.wait_ge(h_hi, j + 1)
                nc.gpsimd.tensor_tensor(hT[:, bass.ds(slot, 1), LO, :, 1:CH + 1], hf[:].unsqueeze(1),
                                        hT[:, bass.ds(slot, 1), HI, :, 1:CH + 1].bitcast(F32),
                                        ALU.subtract).then_inc(h_ready, 1)
                pool.wait_ge(h_ready, 3 * j + 1)
                both = lambda s, col: hT[:, bass.ds(s, 1), :, :, col:col + 1].rearrange("p a b c d -> p (a b c) d")
                kj = keep[:, bass.ds(j, 1), :].rearrange("p a (b c) -> p (a b) c", c=1)
                nc.gpsimd.tensor_tensor(both(slot, 0), both(other, CH).bitcast(F32), kj, ALU.mult).then_inc(h_ready, 1)
                nc.gpsimd.tensor_tensor(both(other, CH + 1), both(slot, 1).bitcast(F32), kj, ALU.mult
                                        ).then_inc(h_ready, 1)

            link(nc.gpsimd.memset(ident[:], 0.0))
            link(nc.gpsimd.affine_select(out=ident[:], in_=ident[:], compare_op=ALU.not_equal, fill=1.0, base=0,
                                         pattern=[[-1, P]], channel_multiplier=1))
            link(nc.gpsimd.memset(half[:], -0.5))
            rstd(0)
            link(nc.gpsimd.tensor_copy(ident16[:], ident[:]))
            link(nc.gpsimd.memset(mask[:], 0.0))
            link(nc.gpsimd.affine_select(out=mask[:], in_=mask[:], compare_op=ALU.is_ge, fill=NEG, base=0,
                                         pattern=[[0, 4], [-1, P]], channel_multiplier=1))
            link(nc.gpsimd.memset(pick[:], 0.0))
            link(nc.gpsimd.affine_select(out=pick[:], in_=pick[:], compare_op=ALU.not_equal, fill=1.0, base=0,
                                         pattern=[[-1, NB], [0, P]], channel_multiplier=1))
            link(nc.gpsimd.memset(keep[:], 1.0))
            for j in range(0, NCH + 2, CPB):
                link(nc.gpsimd.memset(keep[:, j, :], 0.0))
            link(nc.gpsimd.memset(hT[:, 1, :, :, CH:CH + 1].bitcast(F32), 0.0))
            link(nc.gpsimd.iota(iota[:], pattern=[[1, E]], base=0, channel_multiplier=0,
                                allow_small_or_imprecise_dtypes=True))
            assert chain.now() == N_CONST
            for j in range(3):
                if j > 0:
                    rstd(j)
                low_and_halo(j, j % 2, (j + 1) % 2)
            with pool.Fori(0, NCH - 1) as t:
                slot, other = pool.snap((t + 3) % 2), pool.snap(t % 2)
                pool.wait_ge(ld["xr"], 16 * t + 16)
                pool.wait_ge(m_done, N_MOD)
                for b in range(2):
                    nc.gpsimd.tensor_tensor(xr[:, b:b + 1, :], xr[:, b:b + 1, :], gaPB[:, bass.ds(t // CPB, 1), :],
                                            ALU.add).then_inc(xr_biased, 1)
                rstd(t + 3)
                low_and_halo(t + 3, slot, other)
            pool.wait_ge(ld["xr"], 16 * NCH)
            for b in range(2):
                nc.gpsimd.tensor_tensor(xr[:, b, :], xr[:, b, :], gaPB[:, NB - 1, :], ALU.add).then_inc(xr_biased, 1)

            def rstd2(i):
                pool.wait_ge(var2_ready, i + 1)
                nc.gpsimd.tensor_tensor(rs[:, 1, 0:1], rs[:, 0, 0:1], half[:, 0:1], ALU.pow).then_inc(rstd2_ready, 1)

            def bias2(i, slot, b):
                pool.wait_ge(xn2_ready, i + 1)
                nc.gpsimd.tensor_tensor(x2[:, bass.ds(slot, 1), :], x2[:, bass.ds(slot, 1), :],
                                        gbBB[:, bass.ds(b, 1), :], ALU.add).then_inc(x2_biased, 1)

            def low2(i, p):
                pool.wait_ge(h2_hi, i + 1)
                nc.gpsimd.tensor_tensor(h2[:, p, LO], hf2[:, p], h2[:, p, HI].bitcast(F32), ALU.subtract
                                        ).then_inc(h2_ready, 1)

            pool.wait_ge(o_done, PREP_A)
            for i in range(2):
                rstd2(i)
                bias2(i, i, 0)
                low2(i, i)
            with pool.Fori(0, NBLK // 2) as it:
                batch = pool.snap(((2 * it + 2) % NBLK) // BPB)
                for p in range(2):
                    i = 2 * it + p
                    rstd2(i + 2)
                    bias2(i + 2, (i + 2) % 4, batch)
                    low2(i + 2, p)

        @block.scalar
        def _(act):
            for b in range(NB):
                act.dma_start(silT[:, 0, :, b], cond[b].rearrange("(k p) -> p k", p=P),
                               allow_slow_non_contiguous=True).then_inc(ld["c"], 16)
            small = [(cb[:], conv_b.rearrange("(o p) -> p o", p=P)),
                     (bqk[:, 0:NC], bq.rearrange("(c two) e -> (two e) c", two=2)),
                     (bqk[:, NC:], bk.rearrange("(c two) e -> (two e) c", two=2)),
                     (bvT[:], bv.rearrange("(c two) e -> (two e) c", two=2)),
                     (boT[:], bo.rearrange("(p a) -> p a", a=1)),
                     (brow[:], proj_b.rearrange("(a d) -> a d", a=1))]
            assert len(small) == SMALL
            for dst, src in small:
                act.dma_start(dst, src, allow_slow_non_contiguous=True).then_inc(ld["small"], 16)
            act.wait_ge(ld["c"], 16 * NB)
            nc.scalar.activation(silT[:, 1], silT[:, 0], ACT.Exp, scale=-1.0).then_inc(sil_exp, 1)

            def split(n):
                dst, raw, scale, loaded = splits[n]
                act.wait_ge(loaded, 16)
                nc.scalar.activation(dst[:, HI], raw if n < N_SPLIT - 2 else raw[:], ACT.Copy, scale=scale
                                     ).then_inc(split_hi, 1)

            def high(j, slot):
                act.wait_ge(t_done, j_done(j))
                nc.scalar.activation(hT[:, bass.ds(slot, 1), HI, :, 1:CH + 1], hf[:].unsqueeze(1), ACT.Copy
                                     ).then_inc(h_hi, 1)

            def j_done(j):
                return 2 * j + 2 if type(j) is int and j < 3 else t_at(j - 3, T_N)

            def conv_high(index, n):
                act.wait_ge(c_full, index + 1)
                nc.scalar.activation(cv[:, n, HI], CB[:, 0:CH], ACT.Identity, bias=cb[:, n:n + 1]).then_inc(cv_hi, 1)

            def qk_high(index, bank, g):
                act.wait_ge(p_full, index + 1)
                for a in range(2):
                    nc.scalar.activation(qk16[:, HI, 2 * g + a], bank[:, a * CH:(a + 1) * CH], ACT.Identity,
                                         bias=bqk[:, 2 * g + a:2 * g + a + 1]).then_inc(qk_hi, 1)

            def v_high(index, bank, g):
                act.wait_ge(p_full, index + 1)
                nc.scalar.activation(v16[:, HI, g // 2, (g % 2) * 512:(g % 2) * 512 + 512], bank[:], ACT.Copy
                                     ).then_inc(v_hi, 1)

            for n in range(TAPS):
                split(n)
            high(0, 0)
            for n in range(TAPS, N_SPLIT - 2):
                split(n)
            high(1, 1)
            for n in range(N_SPLIT - 2, N_SPLIT):
                split(n)
            act.wait_ge(ld["small"], 16 * SMALL)
            act.wait_ge(split_lo, N_SPLIT + 1)
            for n in range(3):
                conv_high(n, n)
            for g in range(8):
                qk_high(g, S[g % 4], g)
            for g in range(4):
                v_high(8 + g, S[g % 4], g)
            high(2, 0)

            def attend(t, ahead):
                t_use = T_USE if ahead else T_LAST

                def exps(u):
                    for bank in range(2):
                        for i in range(4):
                            if i == 0:
                                act.wait_ge(nm_ready, 8 * t + 2 * u + bank + 1)
                            n = 4 * bank + i
                            ins = nc.scalar.activation(prob[:, u, n], S[2 * (u % 2) + bank][:, i * P:(i + 1) * P],
                                                       ACT.Exp, bias=nm[:, u, n:n + 1],
                                                       accum_out=rsum[:, u, n:n + 1])
                        ins.then_inc(s_done, 1)

                def pt_high(u):
                    for g in range(2):
                        k = t_use["pt", u] + g
                        act.wait_ge(t_full, t_at(t, k) + 1)
                        nc.scalar.activation(pt16[:, u % 2, HI, 4 * g:4 * g + 4], TB[(T0 + k) % 2][:].rearrange(
                            "p (h q) -> p h q", h=4), ACT.Copy).then_inc(pt_hi, 1)

                def ot_high(b):
                    for g in range(2):
                        k = t_use["ot", b] + g
                        act.wait_ge(t_full, t_at(t, k) + 1)
                        nc.scalar.activation(oT[:, HI, 4 * g:4 * g + 4, b * P:(b + 1) * P],
                                             TB[(T0 + k) % 2][:].rearrange("p (h q) -> p h q", h=4), ACT.Copy
                                             ).then_inc(ot_hi, 1)

                conv = 0
                for stage, n in STEP_ACT if ahead else LAST:
                    if stage == "s":
                        exps(n)
                    elif stage == "c":
                        conv += n
                        if conv % (CONV_N // 3) == 0:
                            conv_high(c_at(t, conv // (CONV_N // 3) - 1), conv // (CONV_N // 3) - 1)
                    elif stage == "pt":
                        pt_high(n)
                    elif stage == "ot":
                        ot_high(n)
                    elif stage == "qk":
                        qk_high(p_at(t, P_USE[stage, n]), S[P_USE[stage, n] % 4], n)
                    elif stage == "v":
                        v_high(p_at(t, P_USE[stage, n]), S[P_USE[stage, n] % 4], n)
                    elif stage == "wo":
                        act.wait_ge(w_full, w_at(t, W_USE["wo", 0]) + 1)
                        nc.scalar.activation(att[:, HI], WB[:, 0:CH], ACT.Identity, bias=bofs[:]).then_inc(att_hi, 1)
                    elif stage == "ln":
                        high(t + 3, act.snap((t + 3) % 2))
                    elif stage == "b":
                        prep_high(n)

            def prep_high(n):
                if n < PREP_B:
                    return
                act.wait_ge(o_full, n + 1)
                dst = btw[:, HI, n - PREP_B] if n < PREP_W else bsw[:, HI, n - PREP_W]
                nc.scalar.activation(dst, S[n % 4][:], ACT.Copy).then_inc(prep_hi, 1)

            with act.Fori(0, NCH - 1) as t:
                attend(t, True)
            attend(NCH - 1, False)

            def h2_high(i, p):
                act.wait_ge(l_done, i + 1)
                nc.scalar.activation(h2[:, p, HI], hf2[:, p], ACT.Copy).then_inc(h2_hi, 1)

            def router_exp(i, p):
                act.wait_ge(ng_ready, i + 1)
                nc.scalar.activation(ex[:], AB[p][:, R:ARW], ACT.Exp, bias=ng[:], accum_out=zz[:, 1:2]
                                     ).then_inc(ex_done, 1)
                nc.scalar.activation(zz[:, 2:3], top[:, 1:2], ACT.Exp, bias=ng[:]).then_inc(ex_done, 1)

            def gt_high(i, p):
                for g in range(2):
                    act.wait_ge(g_full, 2 * i + g + 1)
                    nc.scalar.activation(gT[:, p, HI, 4 * g:4 * g + 4], TB[g][:].rearrange("p (c q) -> p c q", c=4),
                                         ACT.Copy).then_inc(gt_hi, 1)

            h2_high(0, 0)
            router_exp(0, 0)
            h2_high(1, 1)
            with act.Fori(0, NBLK // 2) as it:
                for p in range(2):
                    i = 2 * it + p
                    gt_high(i, p)
                    router_exp(i + 1, 1 - p)
                    h2_high(i + 2, p)

        @block.vector
        def _(dve):
            chain = Tally(dve_chain)

            def link(instruction):
                chain.inc(instruction)
                dve.wait_ge(dve_chain, chain.now())

            def newton(n):
                link(nc.vector.tensor_tensor(rs[:, 2, 0:n], rs[:, 1, 0:n], rs[:, 1, 0:n], ALU.mult))
                link(nc.vector.tensor_tensor(rs[:, 3, 0:n], rs[:, 2, 0:n], rs[:, 0, 0:n], ALU.mult))
                link(nc.vector.tensor_scalar(rs[:, 2, 0:n], rs[:, 3, 0:n], -0.5, 1.5, ALU.mult, ALU.add))
                link(nc.vector.tensor_tensor(rs[:, 4, 0:n], rs[:, 2, 0:n], rs[:, 1, 0:n], ALU.mult))

            def norm_a(j):
                dve.wait_ge(ld["x"], 16 * (j + 1))
                for b in range(2):
                    ins = nc.vector.bn_stats(st[:, b], xln[:, b])
                link(ins)
                nc.vector.memset(rs[:, 3, 0:1], 0.0)
                for b in range(2):
                    ins = nc.vector.bn_aggr(mv[:, b], st[:, b])
                link(ins)
                nc.vector.tensor_scalar(rs[:, 0, :], mv[:, :, 1], EPS, None, ALU.add).then_inc(var_ready, 1)

            def norm_b(j):
                dve.wait_ge(rstd_ready, j + 1)
                newton(2)
                if not (type(j) is int and j == 0):
                    dve.wait_ge(t_full, 2 * j if type(j) is int and j < 4 else t_at(j - 4, T_N))
                for b in range(2):
                    nc.vector.tensor_scalar(xn[:, b], xln[:, b], mv[:, b, 0:1], rs[:, 4, b:b + 1],
                                            ALU.subtract, ALU.mult).then_inc(xn_ready, 1)

            def modulate(j, index, parity, batch):
                if not (type(j) is int and j == 0):
                    dve.wait_ge(h_ready, 3 * j)
                for g in range(2):
                    dve.wait_ge(t_full, index + g + 1)
                    for c in range(2):
                        n = 2 * g + c
                        ins = nc.vector.tensor_scalar(
                            hf[:, n, :], TB[(parity + g) % 2][:, c * CH:(c + 1) * CH],
                            modT[:, 1, n, bass.ds(batch, 1)], modT[:, 0, n, bass.ds(batch, 1)],
                            ALU.mult, ALU.add)
                    ins.then_inc(t_done, 1)

            def split_low(n):
                dst, raw, scale, _ = splits[n]
                dve.wait_ge(split_hi, n + 1)
                r = raw if n < N_SPLIT - 2 else raw[:]
                nc.vector.scalar_tensor_tensor(out=dst[:, LO], in0=r, scalar=scale, in1=dst[:, HI].bitcast(F32),
                                               op0=ALU.mult, op1=ALU.subtract).then_inc(split_lo, 1)

            def conv_low(j, n):
                dve.wait_ge(cv_hi, 3 * j + n + 1)
                nc.vector.scalar_tensor_tensor(out=cv[:, n, LO], in0=CB[:, 0:CH], scalar=cb[:, n:n + 1],
                                               in1=cv[:, n, HI].bitcast(F32), op0=ALU.add, op1=ALU.subtract
                                               ).then_inc(c_done, 1)

            def qk_low(bank, j, g):
                dve.wait_ge(qk_hi, 16 * j + 2 * g + 2)
                for a in range(2):
                    c = 2 * g + a
                    ins = nc.vector.scalar_tensor_tensor(out=qk16[:, LO, c], in0=bank[:, a * CH:(a + 1) * CH],
                                                         scalar=bqk[:, c:c + 1], in1=qk16[:, HI, c],
                                                         op0=ALU.add, op1=ALU.subtract)
                ins.then_inc(p_done, 1)

            def v_low(bank, j, g):
                dve.wait_ge(v_hi, 4 * j + g + 1)
                cols = slice((g % 2) * 512, (g % 2) * 512 + 512)
                nc.vector.tensor_tensor(v16[:, LO, g // 2, cols], bank[:], v16[:, HI, g // 2, cols],
                                        ALU.subtract).then_inc(p_done, 1)

            def clamp(g):
                a, b = tmprow[:, 0], tmprow[:, 1]
                link(nc.vector.scalar_tensor_tensor(out=a, in0=g, scalar=-1.0, in1=g, op0=ALU.mult, op1=ALU.max))
                link(nc.vector.tensor_scalar(b, g, 0.0, 2.0, ALU.is_ge, ALU.mult))
                link(nc.vector.tensor_scalar(a, a, 0.25, None, ALU.max))
                return nc.vector.scalar_tensor_tensor(out=g, in0=b, scalar=-1.0, in1=a, op0=ALU.add, op1=ALU.mult)

            norm_a(0)
            dve.wait_ge(sil_exp, 1)
            link(nc.vector.tensor_scalar(silT[:, 2], silT[:, 1], 1.0, None, ALU.add))
            link(nc.vector.reciprocal(silT[:, 1], silT[:, 2]))
            nc.vector.tensor_tensor(silT[:, 3], silT[:, 0], silT[:, 1], ALU.mult).then_inc(sil_done, 1)
            norm_b(0)
            for m in range(2):
                dve.wait_ge(m_full, m + 1)
                nc.vector.tensor_copy(mrow[m], S[m][0:NB, :]).then_inc(m_done, 1)
            norm_a(1)
            dve.wait_ge(m_full, 3)
            link(nc.vector.tensor_copy(modT[:, 0:2], S[2][:, 0:2 * DC * NB].rearrange("p (m k b) -> p m k b", m=2, k=DC)))
            nc.vector.tensor_scalar(modT[:, 1], modT[:, 1], 1.0, None, ALU.add).then_inc(m_done, 1)
            dve.wait_ge(m_done, 3)
            modulate(0, 0, 0, 0)
            norm_b(1)
            for n in range(TAPS):
                split_low(n)
            modulate(1, 2, 0, 0)
            for n in range(TAPS, N_SPLIT - 2):
                split_low(n)
            dve.wait_ge(ld["small"], 16 * SMALL)
            for n in range(N_SPLIT - 2, N_SPLIT):
                split_low(n)
            nc.vector.tensor_scalar(bqk[:, 0:NC], bqk[:, 0:NC], DH ** -0.5, None, ALU.mult).then_inc(split_lo, 1)
            dve.wait_ge(m_full, 4)
            link(nc.vector.tensor_copy(mrow[2], S[3][0:NB, :]))
            clamp(mrow[2]).then_inc(m_done, 1)
            norm_a(2)
            for n in range(3):
                conv_low(0, n)
            for g in range(8):
                qk_low(S[g % 4], 0, g)
                if g % 4 == 3:
                    dve.wait_ge(w_full, g // 4 + 1)
                    nc.vector.tensor_copy(mrow2[g // 4], WB[0:NB, :]).then_inc(w_done, 1)
            for g in range(4):
                v_low(S[g % 4], 0, g)
                if g == 1:
                    dve.wait_ge(w_full, 3)
                    link(nc.vector.tensor_copy(gbrow[:], WB[0:NB, :]))
                    clamp(gbrow[:]).then_inc(w_done, 1)
            dve.wait_ge(w_full, 4)
            link(nc.vector.tensor_copy(modT[:, 2:4], WB[:, 0:2 * DC * NB].rearrange("p (m k b) -> p m k b", m=2, k=DC)))
            nc.vector.tensor_scalar(modT[:, 3], modT[:, 3], 1.0, None, ALU.add).then_inc(w_done, 1)
            norm_b(2)
            for b in range(NB):
                dve.wait_ge(m_full, 5 + b)
                nc.vector.tensor_copy(gaB[:, b], S[b][:]).then_inc(m_done, 1)
            dve.wait_ge(m_done, 4 + NB)
            dve.wait_ge(m_full, 7)
            for b in range(NB):
                nc.vector.tensor_tensor(gaPB[:, b], S[2][:], gaB[:, b], ALU.mult).then_inc(m_done, 1)
            dve.wait_ge(w_full, W0)
            nc.vector.tensor_scalar(bofs[:], WB[:, 0:1], boT[:], None, ALU.add).then_inc(w_done, 1)
            modulate(2, 4, 0, 0)
            CHAIN0, N_NORM = chain.now(), 2 + 4 + 4

            def attend(t, ahead):
                chain.at(CHAIN0 + N_NORM * t)
                t_use = T_USE if ahead else T_LAST

                def maxima(u):
                    for bank in range(2):
                        dve.wait_ge(s_full, 8 * t + 2 * u + bank + 1)
                        nc.vector.tensor_reduce(nm[:, u, 4 * bank:4 * bank + 4],
                                                S[2 * (u % 2) + bank][:].rearrange("p (h k) -> p h k", h=4),
                                                AX.X, ALU.max, negate=True).then_inc(nm_ready, 1)

                def pt_low(u):
                    for g in range(2):
                        k = t_use["pt", u] + g
                        dve.wait_ge(pt_hi, 8 * t + 2 * u + g + 1)
                        nc.vector.tensor_tensor(pt16[:, u % 2, LO, 4 * g:4 * g + 4],
                                                TB[(T0 + k) % 2][:].rearrange("p (h q) -> p h q", h=4),
                                                pt16[:, u % 2, HI, 4 * g:4 * g + 4], ALU.subtract
                                                ).then_inc(t_done, 1)

                def ot_low(b):
                    for g in range(2):
                        k = t_use["ot", b] + g
                        dve.wait_ge(ot_hi, 4 * t + 2 * b + g + 1)
                        part = oT[:, :, 4 * g:4 * g + 4, b * P:(b + 1) * P]
                        nc.vector.tensor_tensor(part[:, LO], TB[(T0 + k) % 2][:].rearrange("p (h q) -> p h q", h=4),
                                                part[:, HI].bitcast(F32), ALU.subtract).then_inc(t_done, 1)

                def normalise(u):
                    b, hf_ = u // 2, u % 2
                    dve.wait_ge(s_done, 8 * t + 2 * u + 2)
                    nc.vector.reciprocal(rinv[:, u], rsum[:, u]).then_inc(dve_chain, 1)
                    chain.k += 1
                    dve.wait_ge(dve_chain, chain.now())
                    dve.wait_ge(w_full, w_at(t, W_USE["pv", u]) + 1)
                    v = lambda ap: ap.rearrange("p (c two e) -> p c two e", two=2, e=DH)
                    r = rinv[:, u, :].rearrange("p (two c) -> p c two", two=2).unsqueeze(3)
                    nc.vector.tensor_tensor(v(o[:, b, hf_ * 512:hf_ * 512 + 512]), v(WB[:]),
                                            r.broadcast_to([P, 4, 2, DH]), ALU.mult).then_inc(w_done, 1)

                def residual(b):
                    if b == 0:
                        dve.wait_ge(xr_biased, 2 * t + 2)
                        bank, full, done, use = CB, c_full, c_done, c_pr(t, ahead)
                    else:
                        bank, full, done, use = WB, w_full, w_done, w_at(t, W_USE["pr", 0])
                    dve.wait_ge(full, use + 1)
                    nc.vector.tensor_tensor(x1[:, b:b + 1, :], bank[:].unsqueeze(1), gaB[:, bass.ds(batch, 1), :],
                                            ALU.mult).then_inc(done, 1)
                    dve.wait_ge(done, use + 1)
                    nc.vector.tensor_tensor(x1[:, b], x1[:, b], xr[:, b], ALU.add).then_inc(x1_ready, 1)

                batch = dve.snap(t // CPB) if ahead else NB - 1
                ln_batch = dve.snap(((t + 3) % NCH) // CPB) if ahead else None
                conv = 0
                for stage, n in STEP if ahead else LAST:
                    if stage == "s":
                        maxima(n)
                    elif stage == "c":
                        conv += n
                        if conv % (CONV_N // 3) == 0:
                            conv_low(t + 1, conv // (CONV_N // 3) - 1)
                    elif stage == "pt":
                        pt_low(n)
                    elif stage == "pv":
                        normalise(n)
                    elif stage == "ot":
                        ot_low(n)
                    elif stage == "qk":
                        qk_low(S[P_USE[stage, n] % 4], t + 1, n)
                    elif stage == "v":
                        v_low(S[P_USE[stage, n] % 4], t + 1, n)
                    elif stage == "na":
                        norm_a(t + 3)
                    elif stage == "nb":
                        norm_b(t + 3)
                    elif stage == "wo":
                        dve.wait_ge(att_hi, t + 1)
                        nc.vector.scalar_tensor_tensor(out=att[:, LO], in0=WB[:, 0:CH], scalar=bofs[:],
                                                       in1=att[:, HI].bitcast(F32), op0=ALU.add, op1=ALU.subtract
                                                       ).then_inc(w_done, 1)
                    elif stage == "ln":
                        modulate(t + 3, t_at(t, T_USE[stage, n]), (T0 + T_USE[stage, n]) % 2, ln_batch)
                    elif stage == "pr":
                        residual(n)
                    elif stage == "na2":
                        norm2_a(n, n, 16, ld_x2[n])
                    elif stage == "nb2":
                        norm2_b(n, n)
                    elif stage == "b":
                        prep_low(n)

            def prep_low(n):
                bank = S[n % 4]
                if n < PREP_A:
                    dve.wait_ge(o_full, n + 1)
                    if n == 0:
                        dve.wait_ge(h_ready, 3 * (NCH + 2))
                    if n % 2 == 0:
                        nc.vector.tensor_copy(gbB[:, n // 2], bank[:]).then_inc(o_done, 1)
                    else:
                        dve.wait_ge(o_done, n)
                        nc.vector.tensor_tensor(gbBB[:, n // 2], bank[:], gbB[:, n // 2], ALU.mult
                                                ).then_inc(o_done, 1)
                elif n > PREP_A:
                    part = btw[:, :, n - PREP_B] if n < PREP_W else bsw[:, :, n - PREP_W]
                    dve.wait_ge(prep_hi, n - PREP_B + 1)
                    nc.vector.tensor_tensor(part[:, LO], bank[:], part[:, HI].bitcast(F32), ALU.subtract
                                            ).then_inc(o_done, 1)
                else:
                    dve.wait_ge(o_full, n + 1)
                    nc.vector.tensor_copy(arT[:], bank[:, 0:DC * ARW].rearrange("p (c a) -> p c a", c=DC)
                                          ).then_inc(o_done, 1)

            def norm2_a(i, slot, loads, lsem):
                dve.wait_ge(lsem, loads)
                xi = x2[:, bass.ds(slot, 1), :]
                link(nc.vector.bn_stats(st[:, 0], xi.rearrange("p a d -> p (a d)")))
                nc.vector.memset(rs[:, 3, 0:1], 0.0)
                link(nc.vector.bn_aggr(mv[:, 0], st[:, 0]))
                nc.vector.tensor_scalar(rs[:, 0, 0:1], mv[:, 0, 1:2], EPS, None, ALU.add).then_inc(var2_ready, 1)

            def norm2_b(i, slot):
                dve.wait_ge(rstd2_ready, i + 1)
                newton(1)
                nc.vector.tensor_scalar(xn2[:].unsqueeze(1), x2[:, bass.ds(slot, 1), :], mv[:, 0, 0:1], rs[:, 4, 0:1],
                                        ALU.subtract, ALU.mult).then_inc(xn2_ready, 1)

            with dve.Fori(0, NCH - 1) as t:
                attend(t, True)
                assert chain.k == N_NORM, chain.k
            attend(NCH - 1, False)
            chain.at(CHAIN0 + N_NORM * (NCH - 1) + chain.k)

            def modulate2(i, p, batch):
                dve.wait_ge(l_full, i + 1)
                for c in range(DC):
                    ins = nc.vector.tensor_scalar(hf2[:, p, c], S[2 + p][:, c * P:(c + 1) * P],
                                                  modT[:, 3, c, bass.ds(batch, 1)], modT[:, 2, c, bass.ds(batch, 1)],
                                                  ALU.mult, ALU.add)
                ins.then_inc(l_done, 1)

            def router(i, p):
                dve.wait_ge(a_full, i + 1)
                logits = AB[p][:, R:ARW]
                nc.vector.tensor_copy(res[:], AB[p][:, 0:R])
                link(nc.vector.max(top[:], logits))
                nc.vector.tensor_scalar(ng[:], top[:, 0:1], -1.0, None, ALU.mult).then_inc(ng_ready, 1)
                dve.wait_ge(ex_done, 2 * i + 2)
                nc.vector.tensor_scalar(zz[:, 3:4], zz[:, 1:2], 1e-6, 1.0, ALU.mult, ALU.add).then_inc(dve_chain, 1)
                nc.vector.max_index(topi[:], top[:], logits).then_inc(a_done, 1)
                chain.k += 1
                dve.wait_ge(dve_chain, chain.now())
                dve.wait_ge(a_done, i + 1)
                link(nc.vector.tensor_tensor(zz[:, 4:5], zz[:, 3:4], zz[:, 2:3], ALU.add))
                nc.vector.tensor_copy(topf[:], topi[:, 0:2]).then_inc(dve_chain, 1)
                chain.k += 1
                link(nc.vector.reciprocal(zz[:, 5:6], zz[:, 4:5]))
                link(nc.vector.tensor_scalar(zz[:, 6:7], zz[:, 5:6], 0.5, None, ALU.mult))
                link(nc.vector.tensor_scalar(cmb[:, 0], iota[:], topf[:, 0:1], zz[:, 6:7], ALU.is_equal, ALU.mult))
                link(nc.vector.tensor_tensor(zz[:, 7:8], zz[:, 6:7], zz[:, 2:3], ALU.mult))
                link(nc.vector.tensor_scalar(cmb[:, 1], iota[:], topf[:, 1:2], zz[:, 7:8], ALU.is_equal, ALU.mult))
                link(nc.vector.tensor_tensor(cmb[:, 0], cmb[:, 0], cmb[:, 1], ALU.add))
                nc.vector.tensor_tensor(G[:], cmb[:, 0].unsqueeze(2).broadcast_to([P, E, R]),
                                        res[:].unsqueeze(1).broadcast_to([P, E, R]), ALU.mult).then_inc(g_ready, 1)

            def gt_low(i, p):
                for g in range(2):
                    dve.wait_ge(gt_hi, 2 * i + g + 1)
                    nc.vector.tensor_tensor(gT[:, p, LO, 4 * g:4 * g + 4], TB[g][:].rearrange("p (c q) -> p c q", c=4),
                                            gT[:, p, HI, 4 * g:4 * g + 4].bitcast(F32), ALU.subtract
                                            ).then_inc(g_done, 1)

            modulate2(0, 0, 0)
            norm2_a(1, 1, 16, ld_x2[1])
            norm2_b(1, 1)
            router(0, 0)
            modulate2(1, 1, 0)
            norm2_a(2, 2, 16, ld_x2[2])
            CHAIN2 = chain.now()
            N_BLK = 2 + 4 + 10
            with dve.Fori(0, NBLK // 4) as it:
                for q in range(4):
                    i, p = 4 * it + q, q % 2
                    chain.at(CHAIN2 + N_BLK * i)
                    norm2_b(i + 2, (q + 2) % 4)
                    gt_low(i, p)
                    router(i + 1, 1 - p)
                    modulate2(i + 2, p, dve.snap(((i + 2) % NBLK) // BPB))
                    norm2_a(i + 3, (q + 3) % 4, 16 * (it + (2 if q >= 1 else 1)), ld_x2[(q + 3) % 4])
                    dve.wait_ge(o_full, N_PREP + i + 1)
                    nc.vector.tensor_tensor(ob[:, p:p + 1, :], S[p][:].unsqueeze(1),
                                            gbB[:, bass.ds(dve.snap(i // BPB), 1), :], ALU.mult).then_inc(o_done, 1)
                    dve.wait_ge(o_done, N_PREP + i + 1)
                    dve.wait_ge(x2_biased, i + 1)
                    nc.vector.tensor_tensor(ob[:, p], ob[:, p], x2[:, q], ALU.add).then_inc(ob_ready, 1)
                    assert chain.k == N_BLK, chain.k

        @block.tensor
        def _(pe):
            def passes(dst, stat, mov, first=True, last=True):
                for n, (a, b) in enumerate(PASSES):
                    ins = nc.tensor.matmul(dst, stat(a), mov(b), start=first and n == 0, stop=last and n == 2)
                return ins

            def conv_steps(slot, index):
                for n in range(3):
                    for tap in range(TAPS):
                        for c in range(DC):
                            for k, (a, b) in enumerate(PASSES):
                                start, stop = tap + c + k == 0, tap == TAPS - 1 and c == DC - 1 and k == 2
                                if start and not (type(index) is int and index + n == 0):
                                    pe.wait_ge(c_done, index + n)
                                ins = nc.tensor.matmul(
                                    CB[:, 0:CH], cw[:, a, tap, c, n * P:(n + 1) * P],
                                    hT[:, bass.ds(slot, 1), b, c, tap:tap + CH].rearrange("p a t -> p (a t)"),
                                    start=start, stop=stop)
                                if stop:
                                    ins.then_inc(c_full, 1)
                                yield

            def run(steps, n):
                for _ in range(n):
                    next(steps)

            def project_qk(bank, g, conv_done):
                pe.wait_ge(c_done, conv_done)
                for a in range(2):
                    c = 2 * g + a
                    n = c // NC
                    ins = passes(bank[:, a * CH:(a + 1) * CH],
                                 lambda s: pw[:, s, n, (c % NC) * P:(c % NC + 1) * P], lambda m: cv[:, n, m])
                ins.then_inc(p_full, 1)

            def project_v(bank, g, conv_done):
                pe.wait_ge(c_done, conv_done)
                ins = passes(bank[:], lambda s: cv[:, 2, s, (g // 2) * P:(g // 2 + 1) * P],
                             lambda m: pw[:, m, 2, (g % 2) * 512:(g % 2) * 512 + 512])
                ins.then_inc(p_full, 1)

            def transpose_chunk(j, index, parity):
                pe.wait_ge(xn_ready, 2 * j + 2)
                for g in range(2):
                    if not (type(index) is int and index + g < 2):
                        pe.wait_ge(t_done, index + g - 1)
                    for c in range(2):
                        for b in range(2):
                            ins = nc.tensor.transpose(TB[(parity + g) % 2][:, c * CH + b * P:c * CH + (b + 1) * P],
                                                      xn[:, b, (2 * g + c) * P:(2 * g + c + 1) * P], ident[:])
                    ins.then_inc(t_full, 1)

            def mod_row(dst, w):
                for k in range(DC):
                    ins = nc.tensor.matmul(dst, silT[:, 3, k, :], w(k), start=k == 0, stop=k == DC - 1)
                return ins

            def mod_columns(bank, rows):
                for i in range(2):
                    for k in range(DC):
                        at = (i * DC + k) * NB
                        ins = nc.tensor.transpose(bank[:, at:at + NB], rows[i][:, k * P:(k + 1) * P],
                                                  ident[0:NB, 0:NB])
                return ins

            pe.wait_ge(pool_chain, 2)
            transpose_chunk(0, 0, 0)
            pe.wait_ge(sil_done, 1)
            pe.wait_ge(ld["wm0"], 16)
            for m in range(2):
                mod_row(S[m][0:NB, :], lambda k: wm[:, k, m, :]).then_inc(m_full, 1)
            pe.wait_ge(m_done, 2)
            mod_columns(S[2], mrow).then_inc(m_full, 1)
            pe.wait_ge(pool_chain, N_CONST)
            transpose_chunk(1, 2, 0)
            pe.wait_ge(ld["wm1"], 16)
            mod_row(S[3][0:NB, :], lambda k: wm[:, k, 2, :]).then_inc(m_full, 1)
            pe.wait_ge(h_ready, 6)
            steps = conv_steps(0, 0)
            pe.wait_ge(split_lo, TAPS)
            run(steps, CONV_N)
            pe.wait_ge(split_lo, N_SPLIT)
            pe.wait_ge(m_done, 3)
            for g in range(8):
                if g == 3:
                    pe.wait_ge(m_done, 4)
                if g >= 4:
                    pe.wait_ge(p_done, g - 3)
                project_qk(S[g % 4], g, 1 + g // 4)
                if g == 3:
                    pe.wait_ge(ld["wm2"], 16)
                if g % 4 == 3:
                    if g == 7:
                        pe.wait_ge(w_done, 1)
                    mod_row(WB[0:NB, :], lambda k: wm[:, k, g // 4, :]).then_inc(w_full, 1)
            for g in range(4):
                pe.wait_ge(p_done, 5 + g)
                project_v(S[g % 4], g, 3)
                if g == 1:
                    pe.wait_ge(w_done, 2)
                    mod_row(WB[0:NB, :], lambda k: wm[:, k, 2, :]).then_inc(w_full, 1)
            pe.wait_ge(w_done, 3)
            mod_columns(WB, mrow2).then_inc(w_full, 1)
            transpose_chunk(2, 4, 0)
            pe.wait_ge(p_done, P0)
            for b in range(NB):
                nc.tensor.matmul(S[b][:], pick[:, b, :], mrow[2], start=True, stop=True).then_inc(m_full, 1)
            pe.wait_ge(ld["small"], 16 * SMALL)
            nc.tensor.matmul(S[2][:], pick[0:1, 0, :], brow[:], start=True, stop=True).then_inc(m_full, 1)
            pe.wait_ge(w_done, 4)
            for c in range(NC):
                for a in range(2):
                    ins = nc.tensor.matmul(WB[:, 0:1], wow[:, a, c, :].bitcast(F32), bvT[:, c:c + 1],
                                           start=c + a == 0, stop=c == NC - 1 and a == 1)
            ins.then_inc(w_full, 1)
            pe.wait_ge(m_done, N_MOD)

            def attend(t, ahead):
                t_use = T_USE if ahead else T_LAST

                def scores(u):
                    b, half_ = u // 2, u % 2
                    use = 8 * t + 2 * u
                    if u >= 2:
                        pe.wait_ge(s_done, use - 2)
                    elif u == 0:
                        pe.wait_ge(p_done, p_at(t, 0) - 2)
                    else:
                        pe.wait_ge(p_done, p_at(t, 0))
                    for bank in range(2):
                        nc.tensor.matmul(S[2 * (u % 2) + bank][:], ident16[:], mask[:].rearrange("p h k -> p (h k)"),
                                         start=True, stop=False)
                    for i in range(4):
                        c = 4 * half_ + i
                        for n, (a, m) in enumerate(PASSES):
                            for bank in range(2):
                                rows = slice(DH * bank, DH * (bank + 1))
                                ins = nc.tensor.matmul(S[2 * (u % 2) + bank][:, i * P:(i + 1) * P],
                                                       qk16[rows, a, c, b * P:(b + 1) * P],
                                                       qk16[rows, m, NC + c, b * P:(b + 1) * P],
                                                       start=False, stop=i == 3 and n == 2)
                                if i == 3 and n == 2:
                                    ins.then_inc(s_full, 1)

                def transpose_p(u):
                    pe.wait_ge(s_done, 8 * t + 2 * u + 2)
                    for g in range(2):
                        k = t_use["pt", u] + g
                        pe.wait_ge(t_done, t_at(t, k) - 1)
                        for i in range(4):
                            ins = nc.tensor.transpose(TB[(T0 + k) % 2][:, i * P:(i + 1) * P],
                                                      prob[:, u, 4 * g + i, :], ident[:])
                        ins.then_inc(t_full, 1)

                def pv(u):
                    b, half_ = u // 2, u % 2
                    pe.wait_ge(w_done, w_at(t, W_USE["pv", u]))
                    pe.wait_ge(t_done, t_at(t, t_use["pt", u] + 2))
                    for n in range(8):
                        head = 2 * (n % 4) + n // 4
                        ins = passes(WB[:, head * DH:(head + 1) * DH],
                                     lambda s: pt16[:, u % 2, s, n, :],
                                     lambda m: v16[:, m, b, (8 * half_ + head) * DH:(8 * half_ + head + 1) * DH])
                    ins.then_inc(w_full, 1)

                def transpose_o(b):
                    pe.wait_ge(w_done, w_at(t, W_USE["pv", 2 * b + 1]) + 1)
                    for g in range(2):
                        k = t_use["ot", b] + g
                        pe.wait_ge(t_done, t_at(t, k) - 1)
                        for i in range(4):
                            c = 4 * g + i
                            ins = nc.tensor.transpose(TB[(T0 + k) % 2][:, i * P:(i + 1) * P],
                                                      o[:, b, c * P:(c + 1) * P], ident[:])
                        ins.then_inc(t_full, 1)

                def out_projection(b):
                    pe.wait_ge(w_done, w_at(t, W_USE["wo", 0]) + 1)
                    if b == 1:
                        bank, full = WB, w_full
                    else:
                        pe.wait_ge(c_done, c_pr(t, ahead))
                        bank, full = CB, c_full
                    passes(bank[:], lambda s: att[:, s, b * P:(b + 1) * P], lambda m: pjw[:, m, :]).then_inc(full, 1)

                if ahead:
                    slot = pe.snap((t + 1) % 2)
                    steps = conv_steps(slot, c_at(t, 0))
                started = False
                for stage, n in STEP if ahead else LAST:
                    if stage == "s":
                        scores(n)
                    elif stage == "c":
                        if not started:
                            pe.wait_ge(h_ready, 3 * t + 9)
                            started = True
                        run(steps, n)
                    elif stage == "pt":
                        transpose_p(n)
                    elif stage == "pv":
                        pv(n)
                    elif stage == "ot":
                        transpose_o(n)
                    elif stage in ("qk", "v"):
                        k = P_USE[stage, n]
                        if k < 4:
                            pe.wait_ge(s_done, 8 * t + 5 + k)
                        else:
                            pe.wait_ge(p_done, p_at(t, k) - 3)
                        if stage == "qk":
                            project_qk(S[k % 4], n, c_at(t, 1 + n // 4))
                        else:
                            project_v(S[k % 4], n, c_at(t, 3))
                    elif stage == "wo":
                        pe.wait_ge(w_done, w_at(t, W_USE[stage, n]))
                        pe.wait_ge(t_done, t_at(t, t_use["ot", 1] + 2))
                        for c in range(NC):
                            ins = passes(WB[:, 0:CH], lambda s: wow[:, s, c, :], lambda m: oT[:, m, c, :],
                                         c == 0, c == NC - 1)
                        ins.then_inc(w_full, 1)
                    elif stage == "ln":
                        transpose_chunk(t + 3, t_at(t, T_USE[stage, n]), (T0 + T_USE[stage, n]) % 2)
                    elif stage == "pr":
                        out_projection(n)
                    elif stage == "b":
                        prepare(n)

            def prepare(n):
                bank = S[n % 4]
                if n < 4:
                    pe.wait_ge(s_done, 8 * (NCH - 1) + 5 + n)
                else:
                    pe.wait_ge(o_done, n - 3)
                if n < PREP_A:
                    if n == 1:
                        pe.wait_ge(ld["brow2"], 16)
                    ins = nc.tensor.matmul(bank[:], pick[:, n // 2, :] if n % 2 == 0 else pick[0:1, 0, :],
                                           gbrow[:] if n % 2 == 0 else brow2[:], start=True, stop=True)
                elif n > PREP_A:
                    if n == PREP_B:
                        pe.wait_ge(ld["braw"], 16 * DC)
                    elif n == PREP_W:
                        pe.wait_ge(ld["raw"], 16)
                    k = n - PREP_B
                    for c in range(DC):
                        src = (braw[:, c, 2 * k:2 * k + 2, :].rearrange("p e r -> p (e r)") if k < ER else
                               bsraw[:, c, (k - ER) * P:(k - ER + 1) * P])
                        ins = nc.tensor.transpose(bank[:, c * P:(c + 1) * P], src, ident[:])
                else:
                    pe.wait_ge(ld["ar"], 16 * 2)
                    for c in range(DC):
                        ins = nc.tensor.transpose(bank[:, c * ARW:(c + 1) * ARW], arraw[:, c * P:(c + 1) * P],
                                                  ident[0:ARW, 0:ARW])
                ins.then_inc(o_full, 1)

            with pe.Fori(0, NCH - 1) as t:
                attend(t, True)
            attend(NCH - 1, False)

            def transpose_x2(i, p):
                pe.wait_ge(xn2_ready, i + 1)
                if not (type(i) is int and i < 2):
                    pe.wait_ge(l_done, i - 1)
                for c in range(DC):
                    ins = nc.tensor.transpose(S[2 + p][:, c * P:(c + 1) * P], xn2[:, c * P:(c + 1) * P], ident[:])
                ins.then_inc(l_full, 1)

            def low_rank(i, p):
                pe.wait_ge(l_done, i + 1)
                if not (type(i) is int and i == 0):
                    pe.wait_ge(a_done, i)
                for c in range(DC):
                    ins = nc.tensor.matmul(AB[p][:, 0:ARW], hf2[:, p, c, :], arT[:, c, :], start=c == 0, stop=c == DC - 1)
                ins.then_inc(a_full, 1)

            def transpose_g(i, p):
                pe.wait_ge(g_ready, i + 1)
                for g in range(2):
                    if not (type(i) is int and i == 0):
                        pe.wait_ge(g_done, 2 * i + g - 1)
                    for c in range(4):
                        k = 4 * g + c
                        ins = nc.tensor.transpose(TB[g][:, c * P:(c + 1) * P],
                                                  G[:, 2 * k:2 * k + 2, :].rearrange("p e r -> p (e r)"), ident[:])
                    ins.then_inc(g_full, 1)

            pe.wait_ge(o_done, N_PREP - 2)
            transpose_x2(0, 0)
            pe.wait_ge(w_done, w_at(NCH, 0))
            low_rank(0, 0)
            pe.wait_ge(o_done, N_PREP - 1)
            transpose_x2(1, 1)
            pe.wait_ge(c_done, c_pr(NCH - 1, False) + 1)
            pe.wait_ge(t_done, t_at(NCH - 1, T_LAST["ot", 1] + 2))
            pe.wait_ge(o_done, N_PREP)
            transpose_g(0, 0)
            with pe.Fori(0, NBLK // 2) as it:
                for p in range(2):
                    i = 2 * it + p
                    pe.wait_ge(h2_ready, i + 1)
                    pe.wait_ge(o_done, N_PREP + i - 1)
                    for c in range(DC):
                        passes(S[p][:], lambda s: h2[:, p, s, c, :], lambda m: bsw[:, m, c, :], c == 0, False)
                    low_rank(i + 1, 1 - p)
                    transpose_x2(i + 2, p)
                    pe.wait_ge(g_done, 2 * i + 2)
                    for c in range(ER):
                        ins = passes(S[p][:], lambda s: gT[:, p, s, c, :], lambda m: btw[:, m, c, :], False, c == ER - 1)
                    ins.then_inc(o_full, 1)
                    transpose_g(i + 1, 1 - p)


_INS = ['L0_attn_inputs', 'L0_attn_conv_w', 'L0_attn_conv_b', 'L0_attn_wq', 'L0_attn_bq', 'L0_attn_wk',
        'L0_attn_bk', 'L0_attn_wv', 'L0_attn_bv', 'L0_attn_wo', 'L0_attn_bo', 'L0_attn_proj_w',
        'L0_attn_proj_b', 'L0_ffn_base_w', 'L0_ffn_base_b', 'L0_ffn_A', 'L0_ffn_B', 'L0_ffn_router_w',
        'L0_c', 'L0_wmod']
_OUTS = [((2, 1024, 512), 'float32')]


def kernel(**inputs):
    import numpy as _np
    import concourse.bacc as _bacc
    from concourse import mybir as _mybir
    from concourse.bass_utils import run_bass_kernel_spmd as _run

    nc = _bacc.Bacc("TRN2", target_bir_lowering=False, num_devices=1)
    arrays, args = {}, []
    for name in _INS:
        a = _np.ascontiguousarray(inputs[name])
        arrays[f"in_{name}_dram"] = a
        args.append(nc.dram_tensor(f"in_{name}_dram", a.shape, _mybir.dt.from_np(a.dtype), kind="ExternalInput").ap())
    for i, (shape, dtype) in enumerate(_OUTS):
        dt = _mybir.dt.from_np(_np.dtype(dtype))
        args.append(nc.dram_tensor(f"out_{i}_dram", shape, dt, kind="ExternalOutput").ap())
    bass_adaln_block(nc, *args)
    r = _run(nc, [arrays], core_ids=[0])
    got = tuple(r.results[0][f"out_{i}_dram"] for i in range(len(_OUTS)))
    return got[0]
```
